# Optimizing a Trainium2 kernel written in Bass

```python
import numpy as np
import jax
import jax.numpy as jnp

def _softmax(x, axis=-1):
    return jax.nn.softmax(x, axis=axis)

def _gelu(x):
    return jax.nn.gelu(x, approximate=True)

def _silu(x):
    return jax.nn.silu(x)

def _sigmoid(x):
    return jax.nn.sigmoid(x)

def _layernorm(x, axis=-1, eps=1e-05):
    m = jnp.mean(x, axis=axis, keepdims=True)
    v = jnp.var(x, axis=axis, keepdims=True)
    return (x - m) / jnp.sqrt(v + eps)

def _scatter_add(tgt, idx, src, axis=0):
    return tgt.at[idx].add(src)

def _segment_sum(src, seg, n):
    return jax.ops.segment_sum(src, seg, n)
kernel_name = 'mk_prb_d1_jaxref_r8_d067e6'

def setup_inputs(seed: int=0):
    np.random.seed(seed)
    _w = jnp.asarray

    def _L0_attn_setup():
        import jax, jax.numpy as jnp
        import numpy as np
        N_HEADS = 16
        D_HEAD = 128
        D_MODEL = 256
        MAXLEN = 256
        key = jax.random.key(seed)
        ks = jax.random.split(key, 9)
        b, t = (2, 256)
        hd = N_HEADS * D_HEAD
        init = 0.02
        return {'x': jax.random.normal(ks[0], (b, t, D_MODEL), dtype=jnp.float32), 'Wq': jax.random.normal(ks[1], (D_MODEL, hd), dtype=jnp.float32) * init, 'bq': jnp.zeros((hd,), dtype=jnp.float32), 'Wk': jax.random.normal(ks[2], (D_MODEL, hd), dtype=jnp.float32) * init, 'bk': jnp.zeros((hd,), dtype=jnp.float32), 'Wv': jax.random.normal(ks[3], (D_MODEL, hd), dtype=jnp.float32) * init, 'bv': jnp.zeros((hd,), dtype=jnp.float32), 'Wo': jax.random.normal(ks[4], (hd, D_MODEL), dtype=jnp.float32) * init, 'bo': jnp.zeros((D_MODEL,), dtype=jnp.float32)}
    _L0_attn_in = _L0_attn_setup()

    def _L0_ffn_setup():
        import jax, jax.numpy as jnp
        import numpy as np
        BLOCK_SIZE = 32
        HIDDEN_SIZE = 256
        MLP_DIM = 2048
        NVFP4_LUT = jnp.array([0.0, 0.5, 1.0, 1.5, 2.0, 3.0, 4.0, 6.0, 0.0, -0.5, -1.0, -1.5, -2.0, -3.0, -4.0, -6.0], dtype=jnp.float32)

        def dequant_nvfp4(W_packed, scales, block=BLOCK_SIZE):
            N = W_packed.shape[0]
            low = W_packed & 15
            high = W_packed >> 4 & 15
            idx = jnp.stack([low, high], axis=-1).reshape(N, -1)
            vals = NVFP4_LUT[idx]
            K = vals.shape[1]
            vals = vals.reshape(N, K // block, block) * scales[:, :, None]
            return vals.reshape(N, K)
        key = jax.random.key(seed)
        ks = jax.random.split(key, 7)
        x = jax.random.normal(ks[0], (4, 32, HIDDEN_SIZE), dtype=jnp.float32)
        gate_W_packed = jax.random.randint(ks[1], (MLP_DIM, HIDDEN_SIZE // 2), 0, 32, dtype=jnp.int32)
        gate_scales = jax.random.uniform(ks[2], (MLP_DIM, HIDDEN_SIZE // BLOCK_SIZE), dtype=jnp.float32) * 0.1 + 0.001
        up_W_packed = jax.random.randint(ks[3], (MLP_DIM, HIDDEN_SIZE // 2), 0, 32, dtype=jnp.int32)
        up_scales = jax.random.uniform(ks[4], (MLP_DIM, HIDDEN_SIZE // BLOCK_SIZE), dtype=jnp.float32) * 0.1 + 0.001
        down_W_packed = jax.random.randint(ks[5], (HIDDEN_SIZE, MLP_DIM // 2), 0, 32, dtype=jnp.int32)
        down_scales = jax.random.uniform(ks[6], (HIDDEN_SIZE, MLP_DIM // BLOCK_SIZE), dtype=jnp.float32) * 0.1 + 0.001
        return {'x': x, 'gate_W_packed': gate_W_packed, 'gate_scales': gate_scales, 'up_W_packed': up_W_packed, 'up_scales': up_scales, 'down_W_packed': down_W_packed, 'down_scales': down_scales}
    _L0_ffn_in = _L0_ffn_setup()
    _d = {'L0_attn_x': _L0_attn_in['x'], 'L0_attn_Wq': _L0_attn_in['Wq'], 'L0_attn_bq': _L0_attn_in['bq'], 'L0_attn_Wk': _L0_attn_in['Wk'], 'L0_attn_bk': _L0_attn_in['bk'], 'L0_attn_Wv': _L0_attn_in['Wv'], 'L0_attn_bv': _L0_attn_in['bv'], 'L0_attn_Wo': _L0_attn_in['Wo'], 'L0_attn_bo': _L0_attn_in['bo'], 'L0_ffn_gate_W_packed': _L0_ffn_in['gate_W_packed'], 'L0_ffn_gate_scales': _L0_ffn_in['gate_scales'], 'L0_ffn_up_W_packed': _L0_ffn_in['up_W_packed'], 'L0_ffn_up_scales': _L0_ffn_in['up_scales'], 'L0_ffn_down_W_packed': _L0_ffn_in['down_W_packed'], 'L0_ffn_down_scales': _L0_ffn_in['down_scales']}
    _x0 = _d['L0_attn_x']
    _d['L0_attn_x'] = jax.random.normal(jax.random.fold_in(jax.random.key(seed), 1), (2, 1024, 256), dtype=_x0.dtype)
    del _x0
    return _d

def reference(L0_attn_x, L0_attn_Wq, L0_attn_bq, L0_attn_Wk, L0_attn_bk, L0_attn_Wv, L0_attn_bv, L0_attn_Wo, L0_attn_bo, L0_ffn_gate_W_packed, L0_ffn_gate_scales, L0_ffn_up_W_packed, L0_ffn_up_scales, L0_ffn_down_W_packed, L0_ffn_down_scales):

    def _L0_attn_ref(x, Wq, bq, Wk, bk, Wv, bv, Wo, bo):
        import jax, jax.numpy as jnp
        import numpy as np
        N_HEADS = 16
        D_HEAD = 128
        D_MODEL = 256
        MAXLEN = 256
        b, t, _ = x.shape
        h, dh = (N_HEADS, D_HEAD)
        scale = 1.0 / np.sqrt(dh).astype(np.float32)
        q = (x @ Wq + bq).reshape(b, h, t, dh)
        k = (x @ Wk + bk).reshape(b, t, h, dh).transpose(0, 2, 3, 1)
        v = (x @ Wv + bv).reshape(b, t, h, dh).transpose(0, 2, 1, 3)
        logits = jnp.einsum('bhtd,bhds->bhts', q, k) * scale
        mask = jnp.triu(jnp.full((t, t), -jnp.inf, dtype=x.dtype), k=1)
        weights = jax.nn.softmax(logits + mask, axis=-1)
        out = jnp.einsum('bhts,bhsd->bhtd', weights, v)
        out = out.transpose(0, 2, 1, 3).reshape(b, t, h * dh)
        return out @ Wo + bo

    def _L0_ffn_ref(x, gate_W_packed, gate_scales, up_W_packed, up_scales, down_W_packed, down_scales):
        import jax, jax.numpy as jnp
        import numpy as np
        BLOCK_SIZE = 32
        HIDDEN_SIZE = 256
        MLP_DIM = 2048
        NVFP4_LUT = jnp.array([0.0, 0.5, 1.0, 1.5, 2.0, 3.0, 4.0, 6.0, 0.0, -0.5, -1.0, -1.5, -2.0, -3.0, -4.0, -6.0], dtype=jnp.float32)

        def dequant_nvfp4(W_packed, scales, block=BLOCK_SIZE):
            N = W_packed.shape[0]
            low = W_packed & 15
            high = W_packed >> 4 & 15
            idx = jnp.stack([low, high], axis=-1).reshape(N, -1)
            vals = NVFP4_LUT[idx]
            K = vals.shape[1]
            vals = vals.reshape(N, K // block, block) * scales[:, :, None]
            return vals.reshape(N, K)
        B, S, H = x.shape
        xt = x.reshape(B * S, H)
        Wg = dequant_nvfp4(gate_W_packed, gate_scales)
        Wu = dequant_nvfp4(up_W_packed, up_scales)
        Wd = dequant_nvfp4(down_W_packed, down_scales)
        gate = jnp.einsum('th,nh->tn', xt, Wg)
        up = jnp.einsum('th,nh->tn', xt, Wu)
        gelu = jnp.tanh(0.7978845608028654 * (gate + 0.044715 * gate ** 3)) * gate * 0.5 + gate * 0.5
        inter = gelu * up
        out = jnp.einsum('tn,hn->th', inter, Wd)
        return out.reshape(B, S, H)
    x = L0_attn_x
    xn = _layernorm(x, axis=-1)
    x = x + _L0_attn_ref(xn, L0_attn_Wq, L0_attn_bq, L0_attn_Wk, L0_attn_bk, L0_attn_Wv, L0_attn_bv, L0_attn_Wo, L0_attn_bo) + _L0_ffn_ref(xn, L0_ffn_gate_W_packed, L0_ffn_gate_scales, L0_ffn_up_W_packed, L0_ffn_up_scales, L0_ffn_down_W_packed, L0_ffn_down_scales)
    return x

_drawn_inputs = setup_inputs


def setup_inputs(seed=0):
    import zlib

    import numpy as np

    out = dict(_drawn_inputs(seed))
    spreads = {'L0_attn_bq': (0.0, 0.8),
     'L0_attn_bk': (0.0, 0.8),
     'L0_attn_bv': (0.0, 0.8),
     'L0_attn_bo': (0.0, 0.8)}
    factors = {'L0_attn_Wq': 8.0, 'L0_attn_Wk': 8.0, 'L0_attn_Wv': 8.0, 'L0_attn_Wo': 8.0}
    for name, (base, spread) in spreads.items():
        noise = np.random.default_rng([zlib.crc32(name.encode()), seed]).standard_normal(out[name].shape)
        drawn = base * np.exp(spread * noise) if base else spread * noise
        out[name] = jnp.asarray(drawn.astype(out[name].dtype))
    for name, factor in factors.items():
        out[name] = (out[name] * factor).astype(out[name].dtype)
    return out
```

```python
from contextlib import ExitStack

import numpy as np
import concourse.bass as bass
from concourse import mybir

F32, F32R = mybir.dt.float32, mybir.dt.float32r
BF16, I32 = mybir.dt.bfloat16, mybir.dt.int32
ACT = mybir.ActivationFunctionType
ALU = mybir.AluOpType
AX = mybir.AxisListType

P = 128
BATCH, SEQ, DM = 2, 1024, 256
TOK = BATCH * SEQ
HEADS, DH = 16, 128
FF = 2048
QBLOCK = 32
KC = DM // P
NT = TOK // P
N = 512
EPS = 1e-5
SCALE = float(np.float32(1.0) / np.sqrt(np.float32(DH)))
GELU_A, GELU_B = 0.7978845608028654, 0.044715
MASKED = -3.0e38


def flat(ap):
    return ap.rearrange("p a b -> p (a b)")


def split_matmul(nc, out, w_hi, w_lo, m_hi, m_lo, start, stop):
    nc.tensor.matmul(out, w_hi, m_hi, start=start, stop=False)
    nc.tensor.matmul(out, w_hi, m_lo, start=False, stop=False)
    return nc.tensor.matmul(out, w_lo, m_hi, start=False, stop=stop)


def wait(eng, sem, count):
    if isinstance(count, int) and count <= 0:
        return
    eng.wait_ge(sem, count)


def norm_and_ffn(nc, sh, d):
    NJ = FF // P
    TC = TOK // N
    BODY = 4 * TC
    GROUPS = BODY // 2
    W6 = 6 * P
    ps, acc, ident = sh["ps"], sh["acc"], sh["ident"]
    xn_hi, xn_lo = sh["xn_hi"], sh["xn_lo"]
    G = [ps[:, i, :] for i in (0, 1)]
    U = [ps[:, i, :] for i in (2, 3)]
    D = ps[:, 4:6, :]
    WT = ps[:, 6:8, :]

    with ExitStack() as c:
        sb = lambda name, shape, dt: c.enter_context(nc.sbuf_tensor(name, shape, dt))
        sem = lambda name: c.enter_context(nc.semaphore(name))
        x_all = sb("x_all", [P, NT, DM], F32)
        stats = sb("stats", [P, NT, 6], F32)
        mean_var = sb("mean_var", [P, NT, 2], F32)
        minus_half = sb("minus_half", [P, NT], F32)
        var_eps = sb("var_eps", [P, NT], F32)
        rstd = sb("rstd", [P, NT], F32)
        xn_rows = sb("xn_rows", [P, 2, 4, DM], F32)
        bo_col = sb("bo_col", [P, KC], F32)
        raw = sb("raw", [P, 2, W6 // 2], I32)
        scales = sb("scales", [P, NJ, W6 // QBLOCK], F32)
        mag = sb("mag", [P, W6], I32)
        sgn = sb("sgn", [P, W6], I32)
        mag_f = sb("mag_f", [P, W6], F32)
        over4 = sb("over4", [P, W6], F32)
        over6 = sb("over6", [P, W6], F32)
        half_sign = sb("half_sign", [P, W6], F32)
        vals = sb("vals", [P, W6], F32)
        w_rows = sb("w_rows", [P, W6], F32)
        offsets = sb("offsets", [P, 3], F32)
        w_hi = sb("w_hi", [P, 4, 6, P], F32R)
        w_lo = sb("w_lo", [P, 4, 6, P], F32R)
        sq = sb("sq", [P, 2, N], F32)
        inner = sb("inner", [P, 2, N], F32)
        th = sb("th", [P, 2, N], F32)
        gated = sb("gated", [P, 2, N], F32)
        hid = sb("hid", [P, 4, N], F32)
        hid_hi = sb("hid_hi", [P, 4, N], F32R)
        hid_lo = sb("hid_lo", [P, 4, N], F32R)

        x_in = [sem(f"x_in{q}") for q in range(4)]
        raw_in = [sem(f"raw_in{s}") for s in range(2)]
        scales_in, bo_in = sem("scales_in"), sem("bo_in")
        offsets_set, stats_done, mean_done, eps_done, rstd_done, rows_done = (
            sem(s) for s in ("offsets_set", "stats_done", "mean_done", "eps_done", "rstd_done", "rows_done"))
        xt_done, xt_hi_done, xt_lo_done = sem("xt_done"), sem("xt_hi_done"), sem("xt_lo_done")
        ints_done, linear_done, vals_done, w_rows_done = (
            sem(s) for s in ("ints_done", "linear_done", "vals_done", "w_rows_done"))
        wt_done, wt_hi_done, wt_lo_done = sem("wt_done"), sem("wt_hi_done"), sem("wt_lo_done")
        gu_done, sq_done, inner_done, th_done, gated_done, hid_done = (
            sem(s) for s in ("gu_done", "sq_done", "inner_done", "th_done", "gated_done", "hid_done"))
        hid_hi_done, hid_lo_done, down_done, acc_done = (
            sem(s) for s in ("hid_hi_done", "hid_lo_done", "down_done", "acc_done"))
        zeroed, made = sem("ident_zeroed"), sem("ident_made")
        block = c.enter_context(nc.Block())

        def load_raw(eng, j, slot):
            wait(eng, ints_done, j - 1)
            if isinstance(j, int):
                j = j % NJ
            row, col = j * P, j * (P // 2)
            dst = raw[:, slot, :]
            eng.dma_start(dst[:, 0:P], d["gate"][bass.ds(row, P), :]).then_inc(raw_in[slot], 16)
            eng.dma_start(dst[:, P:2 * P], d["up"][bass.ds(row, P), :]).then_inc(raw_in[slot], 16)
            eng.dma_start(dst[:, 2 * P:3 * P].rearrange("p (c k) -> p c k", c=2),
                          d["down"].rearrange("(c p) k -> p c k", p=P)[:, :, bass.ds(col, P // 2)]
                          ).then_inc(raw_in[slot], 16)

        @block.sync
        def _(sp):
            load_raw(sp, 0, 0)
            load_raw(sp, 1, 1)
            for q in range(4):
                sp.dma_start(x_all[:, 4 * q:4 * q + 4, :],
                             d["x"].rearrange("(t p) k -> p t k", p=P)[:, 4 * q:4 * q + 4, :]
                             ).then_inc(x_in[q], 16)
            load_raw(sp, 2, 0)

            def body(it):
                for m in range(4):
                    load_raw(sp, it * 4 + (3 + m), (3 + m) % 2)
            body(0)
            with sp.Fori(1, NJ // 4 - 1) as it:
                body(it)
            body(NJ // 4 - 1)

        @block.gpsimd
        def _(pool):
            nc.gpsimd.memset(ident[:], 0.0).then_inc(zeroed, 1)
            nc.gpsimd.memset(minus_half[:], -0.5).then_inc(offsets_set, 1)
            nc.gpsimd.memset(offsets[:, 0:1], -4.0).then_inc(offsets_set, 1)
            nc.gpsimd.memset(offsets[:, 1:2], -12.0).then_inc(offsets_set, 1)
            nc.gpsimd.memset(offsets[:, 2:3], 0.5).then_inc(offsets_set, 1)
            pool.wait_ge(zeroed, 1)
            nc.gpsimd.affine_select(out=ident[:], in_=ident[:], compare_op=ALU.not_equal, fill=1.0, base=0,
                                    pattern=[[-1, P]], channel_multiplier=1).then_inc(made, 1)

            def piece(j, part):
                if part == 0:
                    pool.wait_ge(linear_done, j * 4 + 4)
                    wait(pool, w_rows_done, j)
                    nc.gpsimd.tensor_tensor(vals[:], over4[:], over6[:], ALU.add).then_inc(vals_done, 1)
                elif part == 1:
                    pool.wait_ge(vals_done, j * 3 + 1)
                    nc.gpsimd.tensor_tensor(vals[:], vals[:], mag_f[:], ALU.add).then_inc(vals_done, 1)
                elif part == 2:
                    pool.wait_ge(vals_done, j * 3 + 2)
                    nc.gpsimd.tensor_tensor(vals[:], vals[:], half_sign[:], ALU.mult).then_inc(vals_done, 1)
                else:
                    pool.wait_ge(vals_done, j * 3 + 3)
                    wait(pool, wt_done, j)
                    scale = scales[:, bass.ds(j & (NJ - 1), 1), :].rearrange("p a b -> p b a")
                    nc.gpsimd.tensor_tensor(
                        w_rows[:].rearrange("p (b k) -> p b k", k=QBLOCK),
                        vals[:].rearrange("p (b k) -> p b k", k=QBLOCK),
                        scale.to_broadcast([P, W6 // QBLOCK, QBLOCK]),
                        ALU.mult).then_inc(w_rows_done, 1)

            pool.wait_ge(scales_in, 64)
            for part in range(4):
                piece(0, part)
            pool.wait_ge(eps_done, 1)
            nc.gpsimd.tensor_tensor(rstd[:], var_eps[:], minus_half[:], ALU.pow).then_inc(rstd_done, 1)
            for part in range(4):
                piece(1, part)
            for part in range(2):
                piece(2, part)

            def body(it):
                for kk in range(BODY):
                    pool.wait_ge(hid_hi_done, it * BODY + (kk + 1))
                    nc.gpsimd.tensor_tensor(hid_lo[:, kk % 4, :], hid[:, kk % 4, :],
                                            hid_hi[:, kk % 4, :].bitcast(F32), ALU.subtract
                                            ).then_inc(hid_lo_done, 1)
                    piece(it * 4 + (2 + (kk + 2) // 4), (kk + 2) % 4)
            body(0)
            with pool.Fori(1, NJ // 4) as it:
                body(it)

        @block.scalar
        def _(act):
            act.dma_start(scales[:, :, 0:8], d["gate_scales"].rearrange("(j p) b -> p j b", p=P)
                          ).then_inc(scales_in, 16)
            act.dma_start(scales[:, :, 8:16], d["up_scales"].rearrange("(j p) b -> p j b", p=P)
                          ).then_inc(scales_in, 16)
            for h in range(2):
                act.dma_start(scales[:, :, 16 + 4 * h:20 + 4 * h],
                              d["down_scales"][h * P:(h + 1) * P, :].rearrange("p (j b) -> p j b", b=4)
                              ).then_inc(scales_in, 16)
            act.dma_start(bo_col[:], d["bo"]).then_inc(bo_in, 16)

            def linear(j):
                act.wait_ge(ints_done, j + 1)
                wait(act, vals_done, j * 3)
                nc.scalar.activation(mag_f[:], mag[:], ACT.Copy).then_inc(linear_done, 1)
                nc.scalar.activation(over4[:], mag[:], ACT.Relu, bias=offsets[:, 0:1]).then_inc(linear_done, 1)
                nc.scalar.activation(over6[:], mag[:], ACT.Relu, bias=offsets[:, 1:2], scale=2.0
                                     ).then_inc(linear_done, 1)
                nc.scalar.activation(half_sign[:], sgn[:], ACT.Identity, bias=offsets[:, 2:3], scale=-0.125
                                     ).then_inc(linear_done, 1)

            def weights_high(j, slot, downs):
                act.wait_ge(wt_done, j + 1)
                wait(act, down_done, downs)
                nc.scalar.activation(w_hi[:, slot, :, :].rearrange("p a b -> p (a b)"), flat(WT)[:, 0:W6],
                                     ACT.Copy).then_inc(wt_hi_done, 1)

            act.wait_ge(offsets_set, 4)
            linear(0)
            linear(1)
            for b in range(2 * 4):
                g, ch = divmod(b, KC)
                act.wait_ge(xt_done, b + 1)
                nc.scalar.activation(xn_hi[:, ch, g * N:(g + 1) * N], ps[:, b % 6, :], ACT.Copy
                                     ).then_inc(xt_hi_done, 1)
            weights_high(0, 0, 0)
            linear(2)
            weights_high(1, 1, 0)

            def body(it):
                for kk in range(BODY):
                    k1 = it * BODY + (kk + 1)
                    act.wait_ge(gu_done, k1)
                    nc.scalar.activation(sq[:, kk % 2, :], G[kk % 2], ACT.Square, scale=float(np.sqrt(GELU_B))
                                         ).then_inc(sq_done, 1)
                    act.wait_ge(inner_done, k1)
                    nc.scalar.activation(th[:, kk % 2, :], inner[:, kk % 2, :], ACT.Tanh, scale=GELU_A
                                         ).then_inc(th_done, 1)
                    act.wait_ge(hid_done, k1)
                    wait(act, down_done, it * GROUPS + (kk // 2 - 1))
                    nc.scalar.activation(hid_hi[:, kk % 4, :], hid[:, kk % 4, :], ACT.Copy
                                         ).then_inc(hid_hi_done, 1)
                    if kk % 4 == 2:
                        m = kk // 4
                        weights_high(it * 4 + (2 + m), (2 + m) % 4, it * GROUPS + TC * (m // 2))
                        linear(it * 4 + (3 + m))
            body(0)
            with act.Fori(1, NJ // 4) as it:
                body(it)

        @block.vector
        def _(dve):
            def integers(j, slot):
                dve.wait_ge(raw_in[slot], (j >> 1) * 48 + 48)
                wait(dve, linear_done, j * 4)
                for dst, mask in ((mag, 7), (sgn, 8)):
                    pairs = dst[:].rearrange("p (k two) -> p k two", two=2)
                    nc.vector.tensor_scalar(pairs[:, :, 0], raw[:, slot, :], mask, None, ALU.bitwise_and)
                    last = nc.vector.tensor_scalar(pairs[:, :, 1], raw[:, slot, :], 4, mask,
                                                   ALU.logical_shift_right, ALU.bitwise_and)
                last.then_inc(ints_done, 1)

            def weights_low(j, slot):
                dve.wait_ge(wt_hi_done, j + 1)
                nc.vector.tensor_tensor(w_lo[:, slot, :, :].rearrange("p a b -> p (a b)"), flat(WT)[:, 0:W6],
                                        w_hi[:, slot, :, :].rearrange("p a b -> p (a b)").bitcast(F32),
                                        ALU.subtract).then_inc(wt_lo_done, 1)

            integers(0, 0)
            integers(1, 1)
            for t in range(NT):
                if t % 4 == 0:
                    dve.wait_ge(x_in[t // 4], 16)
                nc.vector.bn_stats(stats[:, t, :], x_all[:, t, :]).then_inc(stats_done, 1)
            for t in range(NT):
                dve.wait_ge(stats_done, t + 1)
                nc.vector.bn_aggr(mean_var[:, t, :], stats[:, t, :]).then_inc(mean_done, 1)
            dve.wait_ge(mean_done, NT)
            nc.vector.tensor_scalar(var_eps[:], mean_var[:, :, 1], EPS, None, ALU.add).then_inc(eps_done, 1)
            dve.wait_ge(rstd_done, 1)
            for t in range(NT):
                if t >= 8 and t % 4 == 0:
                    dve.wait_ge(xt_done, KC * (t // 4 - 1))
                nc.vector.tensor_scalar(xn_rows[:, t // 4 % 2, t % 4, :], x_all[:, t, :], mean_var[:, t, 0:1],
                                        rstd[:, t:t + 1], ALU.subtract, ALU.mult).then_inc(rows_done, 1)
            for b in range(2 * 4):
                g, ch = divmod(b, KC)
                dve.wait_ge(xt_hi_done, b + 1)
                nc.vector.tensor_tensor(xn_lo[:, ch, g * N:(g + 1) * N], ps[:, b % 6, :],
                                        xn_hi[:, ch, g * N:(g + 1) * N].bitcast(F32), ALU.subtract
                                        ).then_inc(xt_lo_done, 1)
            integers(2, 0)
            weights_low(0, 0)
            weights_low(1, 1)
            dve.wait_ge(bo_in, 16)

            def add_down(tc, count, fresh):
                dve.wait_ge(down_done, count)
                cols = slice(tc * N, (tc + 1) * N)
                if fresh:
                    for h in range(KC):
                        last = nc.vector.tensor_scalar(acc[:, h, cols], D[:, h, :], bo_col[:, h:h + 1], None,
                                                       ALU.add)
                else:
                    last = nc.vector.tensor_tensor(acc[:, :, cols], D, acc[:, :, cols], ALU.add)
                last.then_inc(acc_done, 1)

            def body(it, first):
                for kk in range(BODY):
                    s, k1 = kk % 2, it * BODY + (kk + 1)
                    dve.wait_ge(sq_done, k1)
                    nc.vector.scalar_tensor_tensor(inner[:, s, :], sq[:, s, :], 1.0, G[s], ALU.add, ALU.mult
                                                   ).then_inc(inner_done, 1)
                    if kk % 2 == 1 and not (first and kk == 1):
                        add_down((kk - 3) // 2 % TC, it * GROUPS + (kk - 1) // 2, first and kk < 2 * TC + 3)
                    if kk % 4 == 2:
                        integers(it * 4 + (3 + kk // 4), (3 + kk // 4) % 2)
                    dve.wait_ge(th_done, k1)
                    nc.vector.scalar_tensor_tensor(gated[:, s, :], th[:, s, :], 1.0, G[s], ALU.add, ALU.mult
                                                   ).then_inc(gated_done, 1)
                    dve.wait_ge(gated_done, k1)
                    wait(dve, hid_lo_done, it * BODY + (kk - 3))
                    nc.vector.scalar_tensor_tensor(hid[:, kk % 4, :], gated[:, s, :], 0.5, U[s], ALU.mult,
                                                   ALU.mult).then_inc(hid_done, 1)
                    if kk % 4 == 2:
                        weights_low(it * 4 + (2 + kk // 4), (2 + kk // 4) % 4)
            body(0, True)
            with dve.Fori(1, NJ // 4) as it:
                body(it, False)
            add_down(TC - 1, NJ // 4 * GROUPS, False)

        @block.tensor
        def _(pe):
            pe.wait_ge(made, 1)
            for b in range(2 * 4):
                g, ch = divmod(b, KC)
                pe.wait_ge(rows_done, 4 * g + 4)
                wait(pe, xt_lo_done, b - 5)
                for t in range(4):
                    last = nc.tensor.transpose(ps[:, b % 6, t * P:(t + 1) * P],
                                               xn_rows[:, g % 2, t, ch * P:(ch + 1) * P], ident[:])
                last.then_inc(xt_done, 1)

            def transpose_weights(j):
                pe.wait_ge(w_rows_done, j + 1)
                wait(pe, wt_lo_done, j)
                for b in range(6):
                    last = nc.tensor.transpose(WT[:, b // 4, b % 4 * P:(b % 4 + 1) * P],
                                               w_rows[:, b * P:(b + 1) * P], ident[:])
                last.then_inc(wt_done, 1)

            def gate_up(kk, k, slot, new_chunk):
                s, cols = kk % 2, slice(kk // 2 % TC * N, (kk // 2 % TC + 1) * N)
                if new_chunk is not None:
                    pe.wait_ge(wt_lo_done, new_chunk + 1)
                wait(pe, hid_done, k - 1)
                for bank, first_block in ((G[s], 0), (U[s], 2)):
                    for ch in range(KC):
                        last = split_matmul(nc, bank, w_hi[:, slot, first_block + ch, :],
                                            w_lo[:, slot, first_block + ch, :], xn_hi[:, ch, cols],
                                            xn_lo[:, ch, cols], ch == 0, ch == KC - 1)
                last.then_inc(gu_done, 1)

            def down(kk, k, slot):
                pe.wait_ge(hid_lo_done, k + 1)
                if kk % 2 == 0:
                    wait(pe, acc_done, k // 2 if isinstance(k, int) else k >> 1)
                for h in range(KC):
                    last = split_matmul(nc, D[:, h, :], w_hi[:, slot, 4 + h, :], w_lo[:, slot, 4 + h, :],
                                        hid_hi[:, kk % 4, :], hid_lo[:, kk % 4, :], kk % 2 == 0, kk % 2 == 1)
                if kk % 2 == 1:
                    last.then_inc(down_done, 1)

            slot_of = lambda kk: kk // (2 * TC) % 2 * 2 + kk % 2
            pe.wait_ge(xt_lo_done, 2 * 4)
            transpose_weights(0)
            transpose_weights(1)

            def body(it, first):
                for kk in range(BODY):
                    k = it * BODY + kk
                    fresh = kk // 2 % TC == 0
                    gate_up(kk, k, slot_of(kk), it * 4 + slot_of(kk) if fresh else None)
                    if not (first and kk < 2):
                        down((kk - 2) % BODY, it * BODY + (kk - 2), slot_of((kk - 2) % BODY))
                    if kk % 4 == 2:
                        transpose_weights(it * 4 + (2 + kk // 4))
            body(0, True)
            with pe.Fori(1, NJ // 4) as it:
                body(it, False)
            for kk in (BODY - 2, BODY - 1):
                down(kk, (NJ // 4 - 1) * BODY + kk, slot_of(kk))


def attention(nc, sh, d):
    GROUP = N // (SEQ // HEADS)
    GROUPS = BATCH * HEADS // GROUP
    PAIRS = GROUP // 2
    TILES = SEQ // P
    CHUNKS = 12
    QT = N // P
    QUARTER = 2 * P
    SPLITS = 2 * GROUP + 1
    LOADS = 4
    LAG = 3
    ps, acc, ident = sh["ps"], sh["acc"], sh["ident"]
    xn_hi, xn_lo = sh["xn_hi"], sh["xn_lo"]
    S = [ps[:, 0:2, :], ps[:, 2:4, :]]
    O, M = ps[:, 4, :], ps[:, 5, :]
    T = [ps[:, 6, :], ps[:, 7, :]]

    with ExitStack() as c:
        sb = lambda name, shape, dt: c.enter_context(nc.sbuf_tensor(name, shape, dt))
        sem = lambda name: c.enter_context(nc.semaphore(name))
        ident_b = sb("ident_b", [P, P], BF16)
        mask_b = sb("mask_b", [P, P], BF16)
        minus_one = sb("minus_one", [P, 1], F32)
        bq, bk, bv = (sb(name, [P, HEADS], F32) for name in ("bq", "bk", "bv"))
        kv_in = sb("kv_in", [P, KC, 2 * DH], F32)
        kv_hi, kv_lo = sb("kv_hi", [P, KC, 2 * DH], F32R), sb("kv_lo", [P, KC, 2 * DH], F32R)
        wo_in = sb("wo_in", [P, 2, DM], F32)
        wo_hi, wo_lo = sb("wo_hi", [P, 2, DM], F32R), sb("wo_lo", [P, 2, DM], F32R)
        wq_in = sb("wq_in", [P, LOADS, KC, DH], F32)
        wq_hi, wq_lo = sb("wq_hi", [P, LOADS, KC, DH], F32R), sb("wq_lo", [P, LOADS, KC, DH], F32R)
        q_all = sb("q_all", [P, GROUP, SEQ // HEADS, HEADS], F32)
        q_hi, q_lo = sb("q_hi", [P, 2, N], F32R), sb("q_lo", [P, 2, N], F32R)
        k_hi, k_lo = sb("k_hi", [P, 2, SEQ], F32R), sb("k_lo", [P, 2, SEQ], F32R)
        v_hi, v_lo = (sb(name, [P, 2, TILES, DH], F32R) for name in ("v_hi", "v_lo"))
        v_t = sb("v_t", [P, 2, N], F32)
        probs = sb("probs", [P, 4, SEQ], F32)
        neg_max, row_sum, inv_sum = (sb(name, [P, 2 * TILES], F32) for name in ("neg_max", "row_sum", "inv_sum"))
        pt_hi, pt_lo = (sb(name, [P, 2, TILES, QUARTER], F32R) for name in ("pt_hi", "pt_lo"))
        o_hi, o_lo = sb("o_hi", [P, N], F32R), sb("o_lo", [P, N], F32R)

        bias_in, kv_loaded, wo_loaded = sem("bias_in"), sem("kv_loaded"), sem("wo_loaded")
        wq_loaded = [sem(f"wq_loaded{s}") for s in range(LOADS)]
        masks_zeroed, masks_made = sem("masks_zeroed"), sem("masks_made")
        wq_hi_done, wq_lo_done, qp_done, q_done = (sem(s) for s in ("wq_hi_done", "wq_lo_done", "qp_done", "q_done"))
        kv_hi_done, kv_lo_done = sem("kv_hi_done"), sem("kv_lo_done")
        wo_hi_done, wo_lo_done = sem("wo_hi_done"), sem("wo_lo_done")
        q_hi_done, q_lo_done = sem("q_hi_done"), sem("q_lo_done")
        scores_done, max_done, exp_done, inv_done, probs_done = (
            sem(s) for s in ("scores_done", "max_done", "exp_done", "inv_done", "probs_done"))
        pt_done, pt_hi_done, pt_lo_done = sem("pt_done"), sem("pt_hi_done"), sem("pt_lo_done")
        pv_done, o_hi_done, o_lo_done = sem("pv_done"), sem("o_hi_done"), sem("o_lo_done")
        job_done, job_hi_done, job_lo_done = sem("job_done"), sem("job_hi_done"), sem("job_lo_done")
        block = c.enter_context(nc.Block())

        JOBS = ["K0", "O0a", "K1", "O0b", "V0", "V1", "Vt0", "O1a", "Vt1", "O1b"]
        ON_SCALAR = ["K0", "K1", "V0", "V1", "Vt0", "Vt1"]
        ON_VECTOR = ["K0", "O0a", "K1", "O0b", "Vt0", "O1a", "Vt1", "O1b"]
        OUTPUT_AT = {1: "O0a", 2: "O0b", 5: "O1a", 6: "O1b"}
        EARLY_AT = {3: "V0"}
        LATE_AT = {0: "K0", 1: "K1", 3: "V1", 4: "Vt0", 5: "Vt1"}
        FIRST_JOBS = ON_SCALAR
        OUTPUTS = 4
        chunk_of = lambda i: i if i < QT else 2 * i - QT
        banks_of = lambda i: 1 if i < QT else 2

        class Pair:

            def __init__(self, o, p):
                self.o, self.p = o, p
                self.first = isinstance(p, int) and p == 0

            def count(self, k, c):
                if self.first and c <= 0:
                    return 0
                return self.o * (GROUP * k) + self.p * (2 * k) + c

            def head(self, par):
                return self.o * GROUP + self.p * 2 + par

            def shift(self, par, job):
                if not (self.first and par == 0):
                    return 0
                return sum(other[0] == "O" for other in JOBS[JOBS.index(job) + 1:])

            def jobs(self, par, job):
                return self.count(len(JOBS), par * len(JOBS) + len(ON_SCALAR) - OUTPUTS + JOBS.index(job) + 1
                                  + self.shift(par, job))

            def hi(self, par, job):
                return self.count(len(ON_SCALAR), (par + 1) * len(ON_SCALAR) + ON_SCALAR.index(job) + 1)

            def lo(self, par, job, before=0):
                return self.count(len(ON_VECTOR), par * len(ON_VECTOR) + 4 - OUTPUTS + ON_VECTOR.index(job) + 1
                                  + self.shift(par, job) - before)

        class Drain(Pair):

            def __init__(self, o):
                self.o, self.p, self.first = o, PAIRS, False

            def jobs(self, par, job):
                return self.count(len(JOBS), len(ON_SCALAR) - OUTPUTS + list(OUTPUT_AT.values()).index(job) + 1)

            def lo(self, par, job, before=0):
                return self.count(len(ON_VECTOR), 4 - OUTPUTS + list(OUTPUT_AT.values()).index(job) + 1 - before)

        def lagging(b, t, lag):
            return None if b.first and t < lag else divmod(t - lag, TILES)

        def loops(eng, group_start, pair, drain):
            with eng.Fori(0, GROUPS) as o:
                group_start(o)
                pair(Pair(o, 0))
                with eng.Fori(1, PAIRS) as p:
                    pair(Pair(o, p))
                drain(Drain(o))

        def q_loop(eng, body):
            for u in range(4):
                body(0, u)
            with eng.Fori(1, HEADS // 4) as four:
                for u in range(4):
                    body(four * 4, u)

        def acc_cols(o, half):
            return bass.ds(((o >> 1) & (BATCH - 1)) * SEQ + half * N, N)

        @block.scalar
        def _(act):
            for dst, name in ((bq, "bq"), (bk, "bk"), (bv, "bv")):
                act.dma_start(dst[:], d[name]).then_inc(bias_in, 16)

            def load_kv(head):
                cols = bass.ds((head & (HEADS - 1)) * DH, DH)
                for part, name in enumerate(("wk", "wv")):
                    act.dma_start(kv_in[:, :, part * DH:(part + 1) * DH],
                                  d[name].rearrange("(c p) n -> p c n", p=P)[:, :, cols]).then_inc(kv_loaded, 16)

            def load_wo(head, slot):
                act.dma_start(wo_in[:, slot, :], d["wo"][bass.ds((head & (HEADS - 1)) * DH, DH), :]).then_inc(wo_loaded, 16)

            def load_wq(block_, slot):
                act.dma_start(wq_in[:, slot, :, :], d["wq"].rearrange("(c p) n -> p c n", p=P)[
                    :, :, bass.ds((block_ & (HEADS - 1)) * DH, DH)]).then_inc(wq_loaded[slot], 16)

            def kv_high(n32):
                act.wait_ge(kv_loaded, n32)
                nc.scalar.activation(flat(kv_hi[:]), flat(kv_in[:]), ACT.Copy).then_inc(kv_hi_done, 1)

            def wo_high(n16, slot):
                act.wait_ge(wo_loaded, n16)
                nc.scalar.activation(wo_hi[:, slot, :], wo_in[:, slot, :], ACT.Copy).then_inc(wo_hi_done, 1)

            load_kv(0)
            for s in range(LOADS - 1):
                load_wq(s, s)
            load_wo(0, 0)
            act.wait_ge(bias_in, 48)
            kv_high(32)
            wo_high(16, 0)
            act.wait_ge(kv_lo_done, 1)
            load_kv(1)
            load_wo(1, 1)

            def evacuate(job, jobs, head, par, waits_for_lo=0):
                act.wait_ge(job_done, jobs)
                half = int(job[-1])
                if job[0] == "K":
                    nc.disable_value_cache = True
                    ins = nc.scalar.activation(k_hi[:, par, half * N:(half + 1) * N], M, ACT.Identity,
                                               bias=bk[:, bass.ds(head & (HEADS - 1), 1)])
                    nc.disable_value_cache = False
                elif job in ("V0", "V1"):
                    ins = nc.scalar.activation(v_t[:, half, :], M, ACT.Copy)
                else:
                    ins = nc.scalar.activation(flat(v_hi[:, par, half * QT:(half + 1) * QT, :]), M, ACT.Copy)
                ins.then_inc(job_hi_done, 1)

            for n, job in enumerate(FIRST_JOBS):
                evacuate(job, n + 1, 0, 0)
                if job == "V1":
                    kv_high(64)
            act.wait_ge(kv_lo_done, 2)
            load_kv(2)

            def q_split(group, m, half, splits):
                rows = q_all[:, bass.ds(m, 1), half * 32:half * 32 + 32, :].rearrange("p a r c -> p (a r c)")
                nc.scalar.activation(q_hi[:, half, :], rows, ACT.Copy).then_inc(q_hi_done, 1)

            def group_start(o):
                def wq_block(before, u):
                    if not (isinstance(before, int) and u == 0):
                        act.wait_ge(wq_lo_done, o * HEADS + (before + u))
                    load_wq(before + (u + LOADS - 1), (u + LOADS - 1) % LOADS)
                    act.wait_ge(wq_loaded[u], (o * HEADS + before) * 4 + 16)
                    if not isinstance(before, int):
                        act.wait_ge(qp_done, o * HEADS + (before + (u + 1 - LOADS)))
                    nc.scalar.activation(flat(wq_hi[:, u, :, :]), flat(wq_in[:, u, :, :]), ACT.Copy
                                         ).then_inc(wq_hi_done, 1)
                q_loop(act, wq_block)
                act.wait_ge(q_done, o * HEADS + HEADS)
                q_split(o, 0, 0, None)

            def pt_high(b, par, i):
                for ch in range(banks_of(i)):
                    at = chunk_of(i) + ch
                    blocks = min(QT, i + 1 - ch * QT)
                    act.wait_ge(pt_done, b.count(CHUNKS, par * CHUNKS + at + 1))
                    nc.scalar.activation(
                        pt_hi[:, i // 2 % 2, ch * QT:ch * QT + blocks, i % 2 * P:(i % 2 + 1) * P],
                        T[at % 2][:, 0:blocks * P].rearrange("p (a b) -> p a b", b=P), ACT.Copy
                    ).then_inc(pt_hi_done, 1)

            def o_high(b, par, half):
                act.wait_ge(pv_done, b.count(4, par * 4 + 2 * half + 2))
                nc.disable_value_cache = True
                nc.scalar.activation(o_hi[:], O, ACT.Identity, bias=bv[:, bass.ds(b.head(par) & (HEADS - 1), 1)]
                                     ).then_inc(o_hi_done, 1)
                nc.disable_value_cache = False

            def exps(b, t):
                act.wait_ge(max_done, b.count(TILES, t + 1))
                width = (t % TILES + 1) * P
                at = t % (2 * TILES)
                nc.scalar.activation(probs[:, t % 4, 0:width], flat(S[t % 2])[:, 0:width], ACT.Exp,
                                     bias=neg_max[:, at:at + 1], accum_out=row_sum[:, at:at + 1]
                                     ).then_inc(exp_done, 1)

            def pair(b):
                for t in range(2 * TILES):
                    par, i = divmod(t, TILES)
                    if i - 1 in LATE_AT:
                        evacuate(LATE_AT[i - 1], b.jobs(par, LATE_AT[i - 1]), b.head(par + 1), 1 - par)
                    if i in (0, 4) and not (b.first and par == 0):
                        o_high(b, par - 1, i // 4)
                    if lagging(b, t, LAG):
                        pt_high(b, *lagging(b, t, LAG))
                    if lagging(b, t, 1):
                        exps(b, t - 1)
                    if i in EARLY_AT:
                        evacuate(EARLY_AT[i], b.jobs(par, EARLY_AT[i]), b.head(par + 1), 1 - par)
                    if i == 0:
                        if not (b.first and par == 0):
                            act.wait_ge(scores_done, b.count(TILES, t))
                        q_split(b.o, b.p * 2 + par, 1, None)
                    if i == 4:
                        act.wait_ge(scores_done, b.count(TILES, t))
                        q_split(b.o, (b.p * 2 + (par + 1)) & (GROUP - 1), 0, None)
                        kv_high(b.count(32, par * 32 + 96))
                    if i == 7:
                        if not (b.first and par == 0):
                            act.wait_ge(job_done, b.jobs(par, "O1b"))
                        wo_high(b.count(16, par * 16 + 32), 1 - par)
                        act.wait_ge(kv_lo_done, b.count(1, par + 3))
                        load_kv(b.head(par + 3))
                        act.wait_ge(wo_lo_done, b.count(1, par + 1))
                        load_wo(b.head(par + 2), par)

            def drain(b):
                o_high(b, -1, 0)
                exps(b, -1)
                for i in range(TILES - LAG, TILES):
                    pt_high(b, -1, i)
                o_high(b, -1, 1)
            loops(act, group_start, pair, drain)
            act.wait_ge(kv_loaded, 32 * (BATCH * HEADS + 3))
            act.wait_ge(wo_loaded, 16 * (BATCH * HEADS + 2))
            for s in range(LOADS):
                act.wait_ge(wq_loaded[s], 16 * (GROUPS * HEADS // LOADS + (s < LOADS - 1)))

        @block.gpsimd
        def _(pool):
            nc.gpsimd.memset(ident_b[:], 0.0).then_inc(masks_zeroed, 1)
            nc.gpsimd.memset(mask_b[:], 0.0).then_inc(masks_zeroed, 1)
            nc.gpsimd.memset(minus_one[:], -1.0).then_inc(masks_zeroed, 1)
            pool.wait_ge(masks_zeroed, 3)
            nc.gpsimd.affine_select(out=ident_b[:], in_=ident_b[:], compare_op=ALU.not_equal, fill=1.0, base=0,
                                    pattern=[[-1, P]], channel_multiplier=1).then_inc(masks_made, 1)
            nc.gpsimd.affine_select(out=mask_b[:], in_=mask_b[:], compare_op=ALU.is_ge, fill=MASKED, base=0,
                                    pattern=[[-1, P]], channel_multiplier=1).then_inc(masks_made, 1)

            def low(dst, src, high, high_done, count, done):
                pool.wait_ge(high_done, count)
                nc.gpsimd.tensor_tensor(dst, src, high.bitcast(F32), ALU.subtract).then_inc(done, 1)

            def kv_low(count):
                low(flat(kv_lo[:]), flat(kv_in[:]), flat(kv_hi[:]), kv_hi_done, count, kv_lo_done)

            def wo_low(count, slot):
                low(wo_lo[:, slot, :], wo_in[:, slot, :], wo_hi[:, slot, :], wo_hi_done, count, wo_lo_done)

            def q_low(m, half, count):
                rows = q_all[:, bass.ds(m, 1), half * 32:half * 32 + 32, :].rearrange("p a r c -> p (a r c)")
                low(q_lo[:, half, :], rows, q_hi[:, half, :], q_hi_done, count, q_lo_done)

            kv_low(1)
            wo_low(1, 0)
            kv_low(2)

            def group_start(o):
                q_loop(pool, lambda before, u: low(
                    flat(wq_lo[:, u, :, :]), flat(wq_in[:, u, :, :]), flat(wq_hi[:, u, :, :]),
                    wq_hi_done, o * HEADS + (before + (u + 1)), wq_lo_done))
                q_low(0, 0, o * SPLITS + 1)

            def pair(b):
                splits = lambda par, half: b.o * SPLITS + b.p * 4 + (2 * par + half + 1)
                for t in range(2 * TILES):
                    par, i = divmod(t, TILES)
                    pool.wait_ge(exp_done, b.count(TILES, t + 1))
                    nc.gpsimd.tensor_tensor(inv_sum[:, t:t + 1], row_sum[:, t:t + 1], minus_one[:], ALU.pow
                                            ).then_inc(inv_done, 1)
                    pool.wait_ge(inv_done, b.count(TILES, t + 1))
                    row = probs[:, t % 4, 0:(i + 1) * P]
                    nc.gpsimd.tensor_tensor(row, row, inv_sum[:, t:t + 1].to_broadcast([P, (i + 1) * P]),
                                            ALU.mult).then_inc(probs_done, 1)
                    if i == 0:
                        q_low(b.p * 2 + par, 1, splits(par, 1))
                    if i == 4:
                        q_low((b.p * 2 + (par + 1)) & (GROUP - 1), 0, splits(par, 2))
                        kv_low(b.count(1, par + 3))
                    if i == 7:
                        wo_low(b.count(1, par + 2), 1 - par)
            loops(pool, group_start, pair, lambda b: None)

        @block.vector
        def _(dve):
            dve.wait_ge(bias_in, 48)

            def evacuate(job, jobs, hi, head, par, o):
                if hi is not None:
                    dve.wait_ge(job_hi_done, hi)
                half = int(job[-1]) if job[0] != "O" else int(job[1])
                if job[0] == "K":
                    cols = slice(half * N, (half + 1) * N)
                    ins = nc.vector.scalar_tensor_tensor(
                        k_lo[:, par, cols], M, bk[:, bass.ds(head & (HEADS - 1), 1)],
                        k_hi[:, par, cols].bitcast(F32), ALU.add, ALU.subtract)
                elif job[0] == "V":
                    blocks = slice(half * QT, (half + 1) * QT)
                    ins = nc.vector.tensor_tensor(flat(v_lo[:, par, blocks, :]), M,
                                                  flat(v_hi[:, par, blocks, :]).bitcast(F32), ALU.subtract)
                else:
                    dve.wait_ge(job_done, jobs)
                    cols = acc[:, "ab".index(job[2]), acc_cols(o, half)]
                    ins = nc.vector.tensor_tensor(cols, M, cols, ALU.add)
                ins.then_inc(job_lo_done, 1)

            for n, job in enumerate(FIRST_JOBS):
                if job not in ("V0", "V1"):
                    evacuate(job, None, n + 1, 0, 0, None)

            def group_start(o):
                def q_block(before, u):
                    dve.wait_ge(qp_done, o * HEADS + (before + (u + 1)))
                    dst = q_all[:].rearrange("p m r c -> p (m r) c")[:, :, bass.ds(before + u, 1)]
                    nc.vector.tensor_scalar(
                        dst.rearrange("p a b -> p (a b)"), S[u % 2][:, 0, :], bq[:, bass.ds(before + u, 1)],
                        SCALE, ALU.add, ALU.mult).then_inc(q_done, 1)
                q_loop(dve, q_block)

            def pt_low(b, par, i):
                for ch in range(banks_of(i)):
                    at = chunk_of(i) + ch
                    blocks = min(QT, i + 1 - ch * QT)
                    dve.wait_ge(pt_hi_done, b.count(CHUNKS, par * CHUNKS + at + 1))
                    where = (slice(None), i // 2 % 2, slice(ch * QT, ch * QT + blocks), slice(i % 2 * P, (i % 2 + 1) * P))
                    nc.vector.tensor_tensor(pt_lo[where], T[at % 2][:, 0:blocks * P].rearrange("p (a b) -> p a b", b=P),
                                            pt_hi[where].bitcast(F32), ALU.subtract).then_inc(pt_lo_done, 1)

            def o_low(b, par, half):
                dve.wait_ge(o_hi_done, b.count(2, par * 2 + half + 1))
                nc.vector.scalar_tensor_tensor(o_lo[:], O, bv[:, bass.ds(b.head(par) & (HEADS - 1), 1)],
                                               o_hi[:].bitcast(F32), ALU.add, ALU.subtract).then_inc(o_lo_done, 1)

            def pair(b):
                for t in range(2 * TILES):
                    par, i = divmod(t, TILES)
                    follows = not (b.first and par == 0)
                    if LATE_AT.get(i - 1) in ON_VECTOR:
                        job = LATE_AT[i - 1]
                        evacuate(job, None, b.hi(par, job), b.head(par + 1), 1 - par, None)
                    if i in (0, 4) and follows:
                        o_low(b, par - 1, i // 4)
                    if lagging(b, t, LAG):
                        pt_low(b, *lagging(b, t, LAG))
                    dve.wait_ge(scores_done, b.count(TILES, t + 1))
                    nc.vector.tensor_reduce(neg_max[:, t:t + 1], flat(S[t % 2])[:, 0:(i + 1) * P], AX.X, ALU.max,
                                            negate=True).then_inc(max_done, 1)
                    if i in OUTPUT_AT and follows:
                        evacuate(OUTPUT_AT[i], b.jobs(par, OUTPUT_AT[i]), None, None, None, b.o)

            def drain(b):
                o_low(b, -1, 0)
                outputs = list(OUTPUT_AT.values())
                for n, i in enumerate(range(TILES - LAG, TILES)):
                    pt_low(b, -1, i)
                    if n < 2:
                        evacuate(outputs[n], b.jobs(0, outputs[n]), None, None, None, b.o)
                o_low(b, -1, 1)
                for job in outputs[2:]:
                    evacuate(job, b.jobs(0, job), None, None, None, b.o)
            loops(dve, group_start, pair, drain)

        @block.tensor
        def _(pe):
            pe.wait_ge(masks_made, 2)

            def project(job, head, weights):
                cols = bass.ds(((head >> 4) & (BATCH - 1)) * SEQ + int(job[1]) * N, N)
                part = slice(0, DH) if job[0] == "K" else slice(DH, 2 * DH)
                pe.wait_ge(kv_lo_done, weights)
                for ch in range(KC):
                    last = split_matmul(nc, M, kv_hi[:, ch, part], kv_lo[:, ch, part], xn_hi[:, ch, cols],
                                        xn_lo[:, ch, cols], ch == 0, ch == KC - 1)
                return last

            def v_rows(half):
                for t in range(QT):
                    last = nc.tensor.transpose(M[:, t * P:(t + 1) * P], v_t[:, half, t * P:(t + 1) * P], ident[:])
                return last

            for n, job in enumerate(FIRST_JOBS):
                if n > 0:
                    done = {"K": job_lo_done, "V": job_hi_done}["V" if FIRST_JOBS[n - 1] in ("V0", "V1") else "K"]
                    pe.wait_ge(done, {1: 1, 2: 2, 3: 3, 4: 4, 5: 3}[n])
                last = v_rows(int(job[-1])) if job[:2] == "Vt" else project(job, 0, 1)
                last.then_inc(job_done, 1)

            def group_start(o):
                def q_block(before, u):
                    pe.wait_ge(wq_lo_done, o * HEADS + (before + (u + 1)))
                    if not (isinstance(before, int) and u < 2):
                        pe.wait_ge(q_done, o * HEADS + (before + (u - 1)))
                    cols = bass.ds(o * N, N)
                    for ch in range(KC):
                        last = split_matmul(nc, S[u % 2][:, 0, :], wq_hi[:, u, ch, :], wq_lo[:, u, ch, :],
                                            xn_hi[:, ch, cols], xn_lo[:, ch, cols], ch == 0, ch == KC - 1)
                    last.then_inc(qp_done, 1)
                q_loop(pe, q_block)

            def scores(b, t):
                par, i = divmod(t, TILES)
                if i == 0 and b.first and par == 0:
                    pe.wait_ge(job_lo_done, b.count(len(ON_VECTOR), 4))
                elif i == 0:
                    pe.wait_ge(job_lo_done, b.lo(par - 1, "K1"))
                if i % QT == 0:
                    pe.wait_ge(q_lo_done, b.o * SPLITS + b.p * 4 + (2 * par + i // QT + 1))
                wait(pe, exp_done, b.count(TILES, t - 1))
                half, cols = i // QT, slice(i % QT * P, (i % QT + 1) * P)
                for bank in range(i // QT + 1):
                    width = min(N, (i + 1) * P - bank * N)
                    keys = slice(bank * N, bank * N + width)
                    diagonal = bank == i // QT
                    last = split_matmul(nc, S[t % 2][:, bank, 0:width], q_hi[:, half, cols], q_lo[:, half, cols],
                                        k_hi[:, par, keys], k_lo[:, par, keys], True, not diagonal)
                    if diagonal:
                        last = nc.tensor.matmul(S[t % 2][:, bank, cols], ident_b[:], mask_b[:], start=False, stop=True)
                last.then_inc(scores_done, 1)

            def transposes(b, par, i, slot):
                pe.wait_ge(probs_done, b.count(TILES, par * TILES + i + 1))
                for ch in range(banks_of(i)):
                    at = chunk_of(i) + ch
                    wait(pe, pt_lo_done, b.count(CHUNKS, par * CHUNKS + at - 1))
                    for n in range(min(QT, i + 1 - ch * QT)):
                        s = ch * QT + n
                        last = nc.tensor.transpose(T[at % 2][:, n * P:(n + 1) * P], probs[:, slot, s * P:(s + 1) * P],
                                                   ident[:])
                    last.then_inc(pt_done, 1)

            def with_v(b, par, q):
                pe.wait_ge(pt_lo_done, b.count(CHUNKS, par * CHUNKS + chunk_of(2 * q + 1) + banks_of(2 * q + 1)))
                if q % 2 == 0:
                    wait(pe, o_lo_done, b.count(2, par * 2 + q // 2))
                for s in range(2 * q + 2):
                    first = P if s == 2 * q + 1 else 0
                    out = O[:, q % 2 * QUARTER + first:(q % 2 + 1) * QUARTER]
                    last = split_matmul(nc, out, v_hi[:, par % 2, s, :], v_lo[:, par % 2, s, :],
                                        pt_hi[:, q % 2, s, first:], pt_lo[:, q % 2, s, first:], s == 0, s == 2 * q + 1)
                last.then_inc(pv_done, 1)

            def output(b, par, half, h):
                pe.wait_ge(o_lo_done, b.count(2, par * 2 + half + 1))
                cols = slice(h * P, (h + 1) * P)
                return split_matmul(nc, M, wo_hi[:, par % 2, cols], wo_lo[:, par % 2, cols], o_hi[:], o_lo[:], True, True)

            def job(b, par, name):
                if name in ("V1", "Vt0"):
                    pe.wait_ge(job_hi_done, b.hi(par, JOBS[JOBS.index(name) - 1]))
                elif name == "V0":
                    pe.wait_ge(job_lo_done, b.lo(par, "K1" if b.first and par == 0 else "O0b"))
                else:
                    pe.wait_ge(job_lo_done, b.lo(par, name, before=1))
                if name in ("K0", "K1", "V0", "V1"):
                    last = project(name, b.head(par + 1), b.count(1, par + 2))
                elif name in ("Vt0", "Vt1"):
                    last = v_rows(int(name[-1]))
                else:
                    if name == "O0a":
                        pe.wait_ge(wo_lo_done, b.count(1, par))
                    last = output(b, par - 1, int(name[1]), "ab".index(name[2]))
                last.then_inc(job_done, 1)

            def pair(b):
                for t in range(2 * TILES):
                    par, i = divmod(t, TILES)
                    if lagging(b, t, LAG):
                        transposes(b, *lagging(b, t, LAG), (t - LAG) % 4)
                    scores(b, t)
                    if i in OUTPUT_AT and not (b.first and par == 0):
                        job(b, par, OUTPUT_AT[i])
                    if i in EARLY_AT:
                        job(b, par, EARLY_AT[i])
                    if t % 2 == 1 and lagging(b, t, LAG + 2):
                        at = lagging(b, t, LAG + 2)
                        with_v(b, at[0], at[1] // 2)
                    if i in LATE_AT:
                        job(b, par, LATE_AT[i])

            def drain(b):
                transposes(b, -1, 5, 5 % 4)
                job(b, 0, "O0a")
                transposes(b, -1, 6, 6 % 4)
                job(b, 0, "O0b")
                with_v(b, -1, 2)
                transposes(b, -1, 7, 7 % 4)
                with_v(b, -1, 3)
                job(b, 0, "O1a")
                job(b, 0, "O1b")
            loops(pe, group_start, pair, drain)


def finish(nc, sh, d, out):
    ps, acc, ident = sh["ps"], sh["acc"], sh["ident"]
    PAIRS = NT // 2
    with ExitStack() as c:
        sem = lambda name: c.enter_context(nc.semaphore(name))
        x_res = c.enter_context(nc.sbuf_tensor("x_res", [P, NT, DM], F32))
        x_res_in = sem("x_res_in")
        out_t_done, out_added, out_stored = sem("out_t_done"), sem("out_added"), sem("out_stored")
        block = c.enter_context(nc.Block())
        rows = lambda dram: dram.rearrange("(t p) k -> p t k", p=P)

        @block.sync
        def _(sp):
            sp.dma_start(x_res[:], rows(d["x"])).then_inc(x_res_in, 16)
            for g in range(PAIRS):
                sp.wait_ge(out_added, g + 1)
                sp.dma_start(rows(out)[:, 2 * g:2 * g + 2, :], x_res[:, 2 * g:2 * g + 2, :]
                             ).then_inc(out_stored, 16)
            sp.wait_ge(out_stored, 16 * PAIRS)

        @block.tensor
        def _(pe):
            for g in range(PAIRS):
                for t in range(2):
                    for h in range(KC):
                        last = nc.tensor.transpose(ps[:, g, (2 * t + h) * P:(2 * t + h + 1) * P],
                                                   acc[:, h, (2 * g + t) * P:(2 * g + t + 1) * P], ident[:])
                last.then_inc(out_t_done, 1)

        @block.vector
        def _(dve):
            dve.wait_ge(x_res_in, 16)
            for g in range(PAIRS):
                dve.wait_ge(out_t_done, g + 1)
                res = flat(x_res[:, 2 * g:2 * g + 2, :])
                nc.vector.tensor_tensor(res, ps[:, g, :], res, ALU.add).then_inc(out_added, 1)


def layer(nc, d, out):
    with ExitStack() as c:
        sb = lambda name, shape, dt: c.enter_context(nc.sbuf_tensor(name, shape, dt))
        sh = {
            "xn_hi": sb("xn_hi", [P, KC, TOK], F32R), "xn_lo": sb("xn_lo", [P, KC, TOK], F32R),
            "acc": sb("acc", [P, KC, TOK], F32), "ident": sb("ident", [P, P], F32),
            "ps": c.enter_context(nc.psum_tensor("ps", [P, 8, N], F32)),
        }
        norm_and_ffn(nc, sh, d)
        attention(nc, sh, d)
        finish(nc, sh, d, out)


def kernel(**inputs):
    import concourse.bacc as bacc
    from concourse.bass_utils import run_bass_kernel_spmd

    names = {
        "x": ("L0_attn_x", (TOK, DM)), "wq": ("L0_attn_Wq", None), "bq": ("L0_attn_bq", None),
        "wk": ("L0_attn_Wk", None), "bk": ("L0_attn_bk", None), "wv": ("L0_attn_Wv", None),
        "bv": ("L0_attn_bv", None), "wo": ("L0_attn_Wo", None), "bo": ("L0_attn_bo", None),
        "gate": ("L0_ffn_gate_W_packed", None), "gate_scales": ("L0_ffn_gate_scales", None),
        "up": ("L0_ffn_up_W_packed", None), "up_scales": ("L0_ffn_up_scales", None),
        "down": ("L0_ffn_down_W_packed", None), "down_scales": ("L0_ffn_down_scales", None),
    }
    nc = bacc.Bacc("TRN2", target_bir_lowering=False, num_devices=1)
    arrays, d = {}, {}
    for short, (name, shape) in names.items():
        a = np.ascontiguousarray(inputs[name])
        if shape is not None:
            a = a.reshape(shape)
        elif a.ndim == 1:
            a = np.ascontiguousarray(a.reshape(-1, P).T)
        arrays[f"in_{short}"] = a
        d[short] = nc.dram_tensor(f"in_{short}", a.shape, mybir.dt.from_np(a.dtype), kind="ExternalInput").ap()
    out = nc.dram_tensor("out", (TOK, DM), F32, kind="ExternalOutput").ap()
    layer(nc, d, out)
    result = run_bass_kernel_spmd(nc, [arrays], core_ids=[0])
    return np.asarray(result.results[0]["out"]).reshape(BATCH, SEQ, DM)
```

```python
from contextlib import ExitStack

import numpy as np
import concourse.bass as bass
from concourse import mybir

F32, F32R = mybir.dt.float32, mybir.dt.float32r
BF16, I32 = mybir.dt.bfloat16, mybir.dt.int32
ACT = mybir.ActivationFunctionType
ALU = mybir.AluOpType
AX = mybir.AxisListType

P = 128
BATCH, SEQ, DM = 2, 1024, 256
TOK = BATCH * SEQ
HEADS, DH = 16, 128
FF = 2048
QBLOCK = 32
KC = DM // P
NT = TOK // P
N = 512
EPS = 1e-5
SCALE = float(np.float32(1.0) / np.sqrt(np.float32(DH)))
GELU_A, GELU_B = 0.7978845608028654, 0.044715
MASKED = -3.0e38


def flat(ap):
    return ap.rearrange("p a b -> p (a b)")


def split_matmul(nc, out, w_hi, w_lo, m_hi, m_lo, start, stop):
    nc.tensor.matmul(out, w_hi, m_hi, start=start, stop=False)
    nc.tensor.matmul(out, w_hi, m_lo, start=False, stop=False)
    return nc.tensor.matmul(out, w_lo, m_hi, start=False, stop=stop)


def wait(eng, sem, count):
    if isinstance(count, int) and count <= 0:
        return
    eng.wait_ge(sem, count)


def norm_and_ffn(nc, sh, d):
    NJ = FF // P
    TC = TOK // N
    BODY = 4 * TC
    GROUPS = BODY // 2
    W6 = 6 * P
    ps, acc, ident = sh["ps"], sh["acc"], sh["ident"]
    xn_hi, xn_lo = sh["xn_hi"], sh["xn_lo"]
    G = [ps[:, i, :] for i in (0, 1)]
    U = [ps[:, i, :] for i in (2, 3)]
    D = ps[:, 4:6, :]
    WT = ps[:, 6:8, :]

    with ExitStack() as c:
        sb = lambda name, shape, dt: c.enter_context(nc.sbuf_tensor(name, shape, dt))
        sem = lambda name: c.enter_context(nc.semaphore(name))
        x_all = sb("x_all", [P, NT, DM], F32)
        stats = sb("stats", [P, NT, 6], F32)
        mean_var = sb("mean_var", [P, NT, 2], F32)
        minus_half = sb("minus_half", [P, NT], F32)
        var_eps = sb("var_eps", [P, NT], F32)
        rstd = sb("rstd", [P, NT], F32)
        xn_rows = sb("xn_rows", [P, 2, 4, DM], F32)
        bo_col = sb("bo_col", [P, KC], F32)
        raw = sb("raw", [P, 2, W6 // 2], I32)
        scales = sb("scales", [P, NJ, W6 // QBLOCK], F32)
        mag = sb("mag", [P, W6], I32)
        sgn = sb("sgn", [P, W6], I32)
        mag_f = sb("mag_f", [P, W6], F32)
        over4 = sb("over4", [P, W6], F32)
        over6 = sb("over6", [P, W6], F32)
        half_sign = sb("half_sign", [P, W6], F32)
        vals = sb("vals", [P, W6], F32)
        w_rows = sb("w_rows", [P, W6], F32)
        offsets = sb("offsets", [P, 3], F32)
        w_hi = sb("w_hi", [P, 4, 6, P], F32R)
        w_lo = sb("w_lo", [P, 4, 6, P], F32R)
        sq = sb("sq", [P, 2, N], F32)
        inner = sb("inner", [P, 2, N], F32)
        th = sb("th", [P, 2, N], F32)
        gated = sb("gated", [P, 2, N], F32)
        hid = sb("hid", [P, 4, N], F32)
        hid_hi = sb("hid_hi", [P, 4, N], F32R)
        hid_lo = sb("hid_lo", [P, 4, N], F32R)

        x_in = [sem(f"x_in{q}") for q in range(4)]
        raw_in = [sem(f"raw_in{s}") for s in range(2)]
        scales_in, bo_in = sem("scales_in"), sem("bo_in")
        offsets_set, stats_done, mean_done, eps_done, rstd_done, rows_done = (
            sem(s) for s in ("offsets_set", "stats_done", "mean_done", "eps_done", "rstd_done", "rows_done"))
        xt_done, xt_hi_done, xt_lo_done = sem("xt_done"), sem("xt_hi_done"), sem("xt_lo_done")
        ints_done, linear_done, vals_done, w_rows_done = (
            sem(s) for s in ("ints_done", "linear_done", "vals_done", "w_rows_done"))
        wt_done, wt_hi_done, wt_lo_done = sem("wt_done"), sem("wt_hi_done"), sem("wt_lo_done")
        gu_done, sq_done, inner_done, th_done, gated_done, hid_done = (
            sem(s) for s in ("gu_done", "sq_done", "inner_done", "th_done", "gated_done", "hid_done"))
        hid_hi_done, hid_lo_done, down_done, acc_done = (
            sem(s) for s in ("hid_hi_done", "hid_lo_done", "down_done", "acc_done"))
        zeroed, made = sem("ident_zeroed"), sem("ident_made")
        block = c.enter_context(nc.Block())

        def load_raw(eng, j, slot):
            wait(eng, ints_done, j - 1)
            if isinstance(j, int):
                j = j % NJ
            row, col = j * P, j * (P // 2)
            dst = raw[:, slot, :]
            eng.dma_start(dst[:, 0:P], d["gate"][bass.ds(row, P), :]).then_inc(raw_in[slot], 16)
            eng.dma_start(dst[:, P:2 * P], d["up"][bass.ds(row, P), :]).then_inc(raw_in[slot], 16)
            eng.dma_start(dst[:, 2 * P:3 * P].rearrange("p (c k) -> p c k", c=2),
                          d["down"].rearrange("(c p) k -> p c k", p=P)[:, :, bass.ds(col, P // 2)]
                          ).then_inc(raw_in[slot], 16)

        @block.sync
        def _(sp):
            load_raw(sp, 0, 0)
            load_raw(sp, 1, 1)
            for q in range(4):
                sp.dma_start(x_all[:, 4 * q:4 * q + 4, :],
                             d["x"].rearrange("(t p) k -> p t k", p=P)[:, 4 * q:4 * q + 4, :]
                             ).then_inc(x_in[q], 16)
            load_raw(sp, 2, 0)

            def body(it):
                for m in range(4):
                    load_raw(sp, it * 4 + (3 + m), (3 + m) % 2)
            body(0)
            with sp.Fori(1, NJ // 4 - 1) as it:
                body(it)
            body(NJ // 4 - 1)

        @block.gpsimd
        def _(pool):
            nc.gpsimd.memset(ident[:], 0.0).then_inc(zeroed, 1)
            nc.gpsimd.memset(minus_half[:], -0.5).then_inc(offsets_set, 1)
            nc.gpsimd.memset(offsets[:, 0:1], -4.0).then_inc(offsets_set, 1)
            nc.gpsimd.memset(offsets[:, 1:2], -12.0).then_inc(offsets_set, 1)
            nc.gpsimd.memset(offsets[:, 2:3], 0.5).then_inc(offsets_set, 1)
            pool.wait_ge(zeroed, 1)
            nc.gpsimd.affine_select(out=ident[:], in_=ident[:], compare_op=ALU.not_equal, fill=1.0, base=0,
                                    pattern=[[-1, P]], channel_multiplier=1).then_inc(made, 1)

            def piece(j, part):
                if part == 0:
                    pool.wait_ge(linear_done, j * 4 + 2)
                    wait(pool, w_rows_done, j)
                    nc.gpsimd.tensor_tensor(vals[:], over4[:], over6[:], ALU.add).then_inc(vals_done, 1)
                elif part == 1:
                    pool.wait_ge(linear_done, j * 4 + 3)
                    pool.wait_ge(vals_done, j * 3 + 1)
                    nc.gpsimd.tensor_tensor(vals[:], vals[:], mag_f[:], ALU.add).then_inc(vals_done, 1)
                elif part == 2:
                    pool.wait_ge(linear_done, j * 4 + 4)
                    pool.wait_ge(vals_done, j * 3 + 2)
                    nc.gpsimd.tensor_tensor(vals[:], vals[:], half_sign[:], ALU.mult).then_inc(vals_done, 1)
                else:
                    pool.wait_ge(vals_done, j * 3 + 3)
                    wait(pool, wt_done, j)
                    scale = scales[:, bass.ds(j & (NJ - 1), 1), :].rearrange("p a b -> p b a")
                    nc.gpsimd.tensor_tensor(
                        w_rows[:].rearrange("p (b k) -> p b k", k=QBLOCK),
                        vals[:].rearrange("p (b k) -> p b k", k=QBLOCK),
                        scale.to_broadcast([P, W6 // QBLOCK, QBLOCK]),
                        ALU.mult).then_inc(w_rows_done, 1)

            pool.wait_ge(scales_in, 64)
            for part in range(4):
                piece(0, part)
            pool.wait_ge(eps_done, 1)
            nc.gpsimd.tensor_tensor(rstd[:], var_eps[:], minus_half[:], ALU.pow).then_inc(rstd_done, 1)
            for part in range(4):
                piece(1, part)
            for part in range(2):
                piece(2, part)

            def body(it):
                for kk in range(BODY):
                    piece(it * 4 + (2 + (kk + 2) // 4), (kk + 2) % 4)
                    pool.wait_ge(hid_hi_done, it * BODY + (kk + 1))
                    nc.gpsimd.tensor_tensor(hid_lo[:, kk % 4, :], hid[:, kk % 4, :],
                                            hid_hi[:, kk % 4, :].bitcast(F32), ALU.subtract
                                            ).then_inc(hid_lo_done, 1)
            body(0)
            with pool.Fori(1, NJ // 4) as it:
                body(it)

        @block.scalar
        def _(act):
            act.dma_start(scales[:, :, 0:8], d["gate_scales"].rearrange("(j p) b -> p j b", p=P)
                          ).then_inc(scales_in, 16)
            act.dma_start(scales[:, :, 8:16], d["up_scales"].rearrange("(j p) b -> p j b", p=P)
                          ).then_inc(scales_in, 16)
            for h in range(2):
                act.dma_start(scales[:, :, 16 + 4 * h:20 + 4 * h],
                              d["down_scales"][h * P:(h + 1) * P, :].rearrange("p (j b) -> p j b", b=4)
                              ).then_inc(scales_in, 16)
            act.dma_start(bo_col[:], d["bo"]).then_inc(bo_in, 16)

            def linear(j, parts):
                for part in parts:
                    if part == 0:
                        act.wait_ge(ints_done, j + 1)
                    wait(act, vals_done, j * 3 - (2, 2, 1, 0)[part])
                    if part == 0:
                        ins = nc.scalar.activation(over4[:], mag[:], ACT.Relu, bias=offsets[:, 0:1])
                    elif part == 1:
                        ins = nc.scalar.activation(over6[:], mag[:], ACT.Relu, bias=offsets[:, 1:2], scale=2.0)
                    elif part == 2:
                        ins = nc.scalar.activation(mag_f[:], mag[:], ACT.Copy)
                    else:
                        ins = nc.scalar.activation(half_sign[:], sgn[:], ACT.Identity, bias=offsets[:, 2:3],
                                                   scale=-0.125)
                    ins.then_inc(linear_done, 1)

            def weights_high(j, slot, downs):
                act.wait_ge(wt_done, j + 1)
                wait(act, down_done, downs)
                nc.scalar.activation(w_hi[:, slot, :, :].rearrange("p a b -> p (a b)"), flat(WT)[:, 0:W6],
                                     ACT.Copy).then_inc(wt_hi_done, 1)

            act.wait_ge(offsets_set, 4)
            linear(0, range(4))
            linear(1, range(4))
            for b in range(2 * 4):
                g, ch = divmod(b, KC)
                act.wait_ge(xt_done, b + 1)
                nc.scalar.activation(xn_hi[:, ch, g * N:(g + 1) * N], ps[:, b % 6, :], ACT.Copy
                                     ).then_inc(xt_hi_done, 1)
            weights_high(0, 0, 0)
            linear(2, range(4))
            weights_high(1, 1, 0)

            def hid_high(it, kk):
                act.wait_ge(hid_done, it * BODY + (kk + 1))
                wait(act, down_done, it * GROUPS + (kk // 2 - 1))
                nc.scalar.activation(hid_hi[:, kk % 4, :], hid[:, kk % 4, :], ACT.Copy
                                     ).then_inc(hid_hi_done, 1)

            def body(it, first):
                for kk in range(BODY):
                    k1 = it * BODY + (kk + 1)
                    act.wait_ge(gu_done, k1)
                    nc.scalar.activation(sq[:, kk % 2, :], G[kk % 2], ACT.Square, scale=float(np.sqrt(GELU_B))
                                         ).then_inc(sq_done, 1)
                    if not (first and kk == 0):
                        hid_high(it, kk - 1)
                    m = kk // 4
                    linear(it * 4 + (3 + m), ((), (0, 1), (2,), (3,))[kk % 4])
                    act.wait_ge(inner_done, k1)
                    nc.scalar.activation(th[:, kk % 2, :], inner[:, kk % 2, :], ACT.Tanh, scale=GELU_A
                                         ).then_inc(th_done, 1)
                    if kk % 4 == 3:
                        weights_high(it * 4 + (2 + m), (2 + m) % 4, it * GROUPS + TC * (m // 2))
            body(0, True)
            with act.Fori(1, NJ // 4) as it:
                body(it, False)
            hid_high(NJ // 4 - 1, BODY - 1)

        @block.vector
        def _(dve):
            def integers(j, slot):
                dve.wait_ge(raw_in[slot], (j >> 1) * 48 + 48)
                wait(dve, linear_done, j * 4)
                for dst, mask in ((mag, 7), (sgn, 8)):
                    pairs = dst[:].rearrange("p (k two) -> p k two", two=2)
                    nc.vector.tensor_scalar(pairs[:, :, 0], raw[:, slot, :], mask, None, ALU.bitwise_and)
                    last = nc.vector.tensor_scalar(pairs[:, :, 1], raw[:, slot, :], 4, mask,
                                                   ALU.logical_shift_right, ALU.bitwise_and)
                last.then_inc(ints_done, 1)

            def weights_low(j, slot):
                dve.wait_ge(wt_hi_done, j + 1)
                nc.vector.tensor_tensor(w_lo[:, slot, :, :].rearrange("p a b -> p (a b)"), flat(WT)[:, 0:W6],
                                        w_hi[:, slot, :, :].rearrange("p a b -> p (a b)").bitcast(F32),
                                        ALU.subtract).then_inc(wt_lo_done, 1)

            integers(0, 0)
            integers(1, 1)
            for t in range(NT):
                if t % 4 == 0:
                    dve.wait_ge(x_in[t // 4], 16)
                nc.vector.bn_stats(stats[:, t, :], x_all[:, t, :]).then_inc(stats_done, 1)
            for t in range(NT):
                dve.wait_ge(stats_done, t + 1)
                nc.vector.bn_aggr(mean_var[:, t, :], stats[:, t, :]).then_inc(mean_done, 1)
            dve.wait_ge(mean_done, NT)
            nc.vector.tensor_scalar(var_eps[:], mean_var[:, :, 1], EPS, None, ALU.add).then_inc(eps_done, 1)
            dve.wait_ge(rstd_done, 1)
            for t in range(NT):
                if t >= 8 and t % 4 == 0:
                    dve.wait_ge(xt_done, KC * (t // 4 - 1))
                nc.vector.tensor_scalar(xn_rows[:, t // 4 % 2, t % 4, :], x_all[:, t, :], mean_var[:, t, 0:1],
                                        rstd[:, t:t + 1], ALU.subtract, ALU.mult).then_inc(rows_done, 1)
            for b in range(2 * 4):
                g, ch = divmod(b, KC)
                dve.wait_ge(xt_hi_done, b + 1)
                nc.vector.tensor_tensor(xn_lo[:, ch, g * N:(g + 1) * N], ps[:, b % 6, :],
                                        xn_hi[:, ch, g * N:(g + 1) * N].bitcast(F32), ALU.subtract
                                        ).then_inc(xt_lo_done, 1)
            integers(2, 0)
            weights_low(0, 0)
            weights_low(1, 1)
            dve.wait_ge(bo_in, 16)

            def add_down(tc, count, fresh):
                dve.wait_ge(down_done, count)
                cols = slice(tc * N, (tc + 1) * N)
                if fresh:
                    for h in range(KC):
                        last = nc.vector.tensor_scalar(acc[:, h, cols], D[:, h, :], bo_col[:, h:h + 1], None,
                                                       ALU.add)
                else:
                    last = nc.vector.tensor_tensor(acc[:, :, cols], D, acc[:, :, cols], ALU.add)
                last.then_inc(acc_done, 1)

            def body(it, first):
                for kk in range(BODY):
                    s, k1 = kk % 2, it * BODY + (kk + 1)
                    dve.wait_ge(sq_done, k1)
                    nc.vector.scalar_tensor_tensor(inner[:, s, :], sq[:, s, :], 1.0, G[s], ALU.add, ALU.mult
                                                   ).then_inc(inner_done, 1)
                    if kk % 2 == 1 and not (first and kk == 1):
                        add_down((kk - 3) // 2 % TC, it * GROUPS + (kk - 1) // 2, first and kk < 2 * TC + 3)
                    if kk % 4 == 0:
                        integers(it * 4 + (3 + kk // 4), (3 + kk // 4) % 2)
                    dve.wait_ge(th_done, k1)
                    nc.vector.scalar_tensor_tensor(gated[:, s, :], th[:, s, :], 1.0, G[s], ALU.add, ALU.mult
                                                   ).then_inc(gated_done, 1)
                    dve.wait_ge(gated_done, k1)
                    wait(dve, hid_lo_done, it * BODY + (kk - 3))
                    nc.vector.scalar_tensor_tensor(hid[:, kk % 4, :], gated[:, s, :], 0.5, U[s], ALU.mult,
                                                   ALU.mult).then_inc(hid_done, 1)
                    if kk % 4 == 3:
                        weights_low(it * 4 + (2 + kk // 4), (2 + kk // 4) % 4)
            body(0, True)
            with dve.Fori(1, NJ // 4) as it:
                body(it, False)
            add_down(TC - 1, NJ // 4 * GROUPS, False)

        @block.tensor
        def _(pe):
            pe.wait_ge(made, 1)
            for b in range(2 * 4):
                g, ch = divmod(b, KC)
                pe.wait_ge(rows_done, 4 * g + 4)
                wait(pe, xt_lo_done, b - 5)
                for t in range(4):
                    last = nc.tensor.transpose(ps[:, b % 6, t * P:(t + 1) * P],
                                               xn_rows[:, g % 2, t, ch * P:(ch + 1) * P], ident[:])
                last.then_inc(xt_done, 1)

            def transpose_weights(j):
                pe.wait_ge(w_rows_done, j + 1)
                wait(pe, wt_lo_done, j)
                for b in range(6):
                    last = nc.tensor.transpose(WT[:, b // 4, b % 4 * P:(b % 4 + 1) * P],
                                               w_rows[:, b * P:(b + 1) * P], ident[:])
                last.then_inc(wt_done, 1)

            def gate_up(kk, k, slot, new_chunk):
                s, cols = kk % 2, slice(kk // 2 % TC * N, (kk // 2 % TC + 1) * N)
                if new_chunk is not None:
                    pe.wait_ge(wt_lo_done, new_chunk + 1)
                wait(pe, hid_done, k - 1)
                for bank, first_block in ((G[s], 0), (U[s], 2)):
                    for ch in range(KC):
                        last = split_matmul(nc, bank, w_hi[:, slot, first_block + ch, :],
                                            w_lo[:, slot, first_block + ch, :], xn_hi[:, ch, cols],
                                            xn_lo[:, ch, cols], ch == 0, ch == KC - 1)
                last.then_inc(gu_done, 1)

            def down(kk, k, slot):
                pe.wait_ge(hid_lo_done, k + 1)
                if kk % 2 == 0:
                    wait(pe, acc_done, k // 2 if isinstance(k, int) else k >> 1)
                for h in range(KC):
                    last = split_matmul(nc, D[:, h, :], w_hi[:, slot, 4 + h, :], w_lo[:, slot, 4 + h, :],
                                        hid_hi[:, kk % 4, :], hid_lo[:, kk % 4, :], kk % 2 == 0, kk % 2 == 1)
                if kk % 2 == 1:
                    last.then_inc(down_done, 1)

            slot_of = lambda kk: kk // (2 * TC) % 2 * 2 + kk % 2
            pe.wait_ge(xt_lo_done, 2 * 4)
            transpose_weights(0)
            transpose_weights(1)

            def body(it, first):
                for kk in range(BODY):
                    k = it * BODY + kk
                    fresh = kk // 2 % TC == 0
                    gate_up(kk, k, slot_of(kk), it * 4 + slot_of(kk) if fresh else None)
                    if not (first and kk < 2):
                        down((kk - 2) % BODY, it * BODY + (kk - 2), slot_of((kk - 2) % BODY))
                    if kk % 4 == 2:
                        transpose_weights(it * 4 + (2 + kk // 4))
            body(0, True)
            with pe.Fori(1, NJ // 4) as it:
                body(it, False)
            for kk in (BODY - 2, BODY - 1):
                down(kk, (NJ // 4 - 1) * BODY + kk, slot_of(kk))


def attention(nc, sh, d):
    GROUP = N // (SEQ // HEADS)
    GROUPS = BATCH * HEADS // GROUP
    PAIRS = GROUP // 2
    TILES = SEQ // P
    CHUNKS = 12
    QT = N // P
    QUARTER = 2 * P
    SPLITS = 2 * GROUP + 1
    LOADS = 4
    WQ_AHEAD = 3
    LAG = 3
    ps, acc, ident = sh["ps"], sh["acc"], sh["ident"]
    xn_hi, xn_lo = sh["xn_hi"], sh["xn_lo"]
    S = [ps[:, 0:2, :], ps[:, 2:4, :]]
    O, M = ps[:, 4, :], ps[:, 5, :]
    T = [ps[:, 6, :], ps[:, 7, :]]

    with ExitStack() as c:
        sb = lambda name, shape, dt: c.enter_context(nc.sbuf_tensor(name, shape, dt))
        sem = lambda name: c.enter_context(nc.semaphore(name))
        ident_b = sb("ident_b", [P, P], BF16)
        mask_b = sb("mask_b", [P, P], BF16)
        minus_one = sb("minus_one", [P, 1], F32)
        bq, bk, bv = (sb(name, [P, HEADS], F32) for name in ("bq", "bk", "bv"))
        kv_in = sb("kv_in", [P, KC, 2 * DH], F32)
        kv_hi, kv_lo = sb("kv_hi", [P, KC, 2 * DH], F32R), sb("kv_lo", [P, KC, 2 * DH], F32R)
        wo_in = sb("wo_in", [P, DM], F32)
        wo_hi, wo_lo = sb("wo_hi", [P, 2, DM], F32R), sb("wo_lo", [P, 2, DM], F32R)
        wq_in = sb("wq_in", [P, LOADS, KC, DH], F32)
        wq_hi, wq_lo = sb("wq_hi", [P, LOADS, KC, DH], F32R), sb("wq_lo", [P, LOADS, KC, DH], F32R)
        q_all = sb("q_all", [P, GROUP, SEQ // HEADS, HEADS], F32)
        q_hi, q_lo = sb("q_hi", [P, 2, N], F32R), sb("q_lo", [P, 2, N], F32R)
        k_hi, k_lo = sb("k_hi", [P, 2, SEQ], F32R), sb("k_lo", [P, 2, SEQ], F32R)
        v_hi, v_lo = (sb(name, [P, 2, TILES, DH], F32R) for name in ("v_hi", "v_lo"))
        v_t = sb("v_t", [P, 2, N], F32)
        probs = sb("probs", [P, 4, SEQ], F32)
        neg_max, row_sum, inv_sum = (sb(name, [P, 2 * TILES], F32) for name in ("neg_max", "row_sum", "inv_sum"))
        pt_hi, pt_lo = (sb(name, [P, 2, TILES, QUARTER], F32R) for name in ("pt_hi", "pt_lo"))
        o_hi, o_lo = sb("o_hi", [P, N], F32R), sb("o_lo", [P, N], F32R)

        bias_in, kv_loaded, wo_loaded = sem("bias_in"), sem("kv_loaded"), sem("wo_loaded")
        wq_loaded = [sem(f"wq_loaded{s}") for s in range(LOADS)]
        masks_zeroed, masks_made = sem("masks_zeroed"), sem("masks_made")
        wq_hi_done, wq_lo_done, qp_done, q_done = (sem(s) for s in ("wq_hi_done", "wq_lo_done", "qp_done", "q_done"))
        kv_hi_done, kv_lo_done = sem("kv_hi_done"), sem("kv_lo_done")
        wo_hi_done, wo_lo_done = sem("wo_hi_done"), sem("wo_lo_done")
        q_hi_done, q_lo_done = sem("q_hi_done"), sem("q_lo_done")
        scores_done, max_done, exp_done, inv_done, probs_done = (
            sem(s) for s in ("scores_done", "max_done", "exp_done", "inv_done", "probs_done"))
        pt_done, pt_hi_done, pt_lo_done = sem("pt_done"), sem("pt_hi_done"), sem("pt_lo_done")
        pv_done, o_hi_done, o_lo_done = sem("pv_done"), sem("o_hi_done"), sem("o_lo_done")
        job_done, job_hi_done, job_lo_done = sem("job_done"), sem("job_hi_done"), sem("job_lo_done")
        block = c.enter_context(nc.Block())

        JOBS = ["K0", "K1", "V0", "O0a", "O0b", "V1", "Vt0", "O1a", "O1b", "Vt1"]
        ON_SCALAR = ["K0", "K1", "V0", "V1", "Vt0", "Vt1"]
        ON_VECTOR = ["K0", "K1", "O0a", "O0b", "Vt0", "O1a", "O1b", "Vt1"]
        FIRST_AT = {0: "K0", 2: "O0a", 6: "O1b", 7: "Vt1"}
        EARLY_AT = {1: "K1", 3: "O0b", 5: "O1a"}
        LATE_AT = {1: "V0", 3: "V1", 4: "Vt0"}
        EAGER = (1, 3, 7)
        FIRST_JOBS = ON_SCALAR
        OUTPUTS = ["O0a", "O0b", "O1a", "O1b"]
        chunk_of = lambda i: i if i < QT else 2 * i - QT
        banks_of = lambda i: 1 if i < QT else 2

        class Pair:

            def __init__(self, o, p):
                self.o, self.p = o, p
                self.first = isinstance(p, int) and p == 0

            def count(self, k, c):
                if self.first and c <= 0:
                    return 0
                return self.o * (GROUP * k) + self.p * (2 * k) + c

            def head(self, par):
                return self.o * GROUP + self.p * 2 + par

            def shift(self, par, job):
                if not (self.first and par == 0):
                    return 0
                return sum(other[0] == "O" for other in JOBS[JOBS.index(job) + 1:])

            def jobs(self, par, job):
                return self.count(len(JOBS), par * len(JOBS) + len(ON_SCALAR) - len(OUTPUTS) + JOBS.index(job) + 1
                                  + self.shift(par, job))

            def hi(self, par, job):
                return self.count(len(ON_SCALAR), (par + 1) * len(ON_SCALAR) + ON_SCALAR.index(job) + 1)

            def lo(self, par, job, before=0):
                return self.count(len(ON_VECTOR), par * len(ON_VECTOR) + 4 - len(OUTPUTS) + ON_VECTOR.index(job) + 1
                                  + self.shift(par, job) - before)

        class Drain(Pair):

            def __init__(self):
                self.o, self.p, self.first = GROUPS - 1, PAIRS, False

            def jobs(self, par, job):
                return self.count(len(JOBS), len(ON_SCALAR) - len(OUTPUTS) + OUTPUTS.index(job) + 1)

            def lo(self, par, job, before=0):
                return self.count(len(ON_VECTOR), 4 - len(OUTPUTS) + OUTPUTS.index(job) + 1 - before)

        def lagging(b, t, lag):
            return None if b.first and t < lag else divmod(t - lag, TILES)

        def loops(eng, group_start, pair, drain):
            group_start(0)
            pair(Pair(0, 0))
            with eng.Fori(1, PAIRS) as p:
                pair(Pair(0, p))
            with eng.Fori(1, GROUPS) as o:
                group_start(o)
                with eng.Fori(0, PAIRS) as p:
                    pair(Pair(o, p))
            drain(Drain())

        def q_loop(eng, body):
            for u in range(4):
                body(0, u)
            with eng.Fori(1, HEADS // 4) as four:
                for u in range(4):
                    body(four * 4, u)

        def acc_cols(head, half):
            return bass.ds(((head >> 4) & (BATCH - 1)) * SEQ + half * N, N)

        @block.scalar
        def _(act):
            for dst, name in ((bq, "bq"), (bk, "bk"), (bv, "bv")):
                act.dma_start(dst[:], d[name]).then_inc(bias_in, 16)

            def load_kv(head):
                cols = bass.ds((head & (HEADS - 1)) * DH, DH)
                for part, name in enumerate(("wk", "wv")):
                    act.dma_start(kv_in[:, :, part * DH:(part + 1) * DH],
                                  d[name].rearrange("(c p) n -> p c n", p=P)[:, :, cols]).then_inc(kv_loaded, 16)

            def load_wo(head):
                act.dma_start(wo_in[:], d["wo"][bass.ds((head & (HEADS - 1)) * DH, DH), :]).then_inc(wo_loaded, 16)

            def load_wq(block_, slot):
                act.dma_start(wq_in[:, slot, :, :], d["wq"].rearrange("(c p) n -> p c n", p=P)[
                    :, :, bass.ds((block_ & (HEADS - 1)) * DH, DH)]).then_inc(wq_loaded[slot], 16)

            def kv_high(n32):
                act.wait_ge(kv_loaded, n32)
                nc.scalar.activation(flat(kv_hi[:]), flat(kv_in[:]), ACT.Copy).then_inc(kv_hi_done, 1)

            def wo_high(n16, slot):
                act.wait_ge(wo_loaded, n16)
                nc.scalar.activation(wo_hi[:, slot, :], wo_in[:], ACT.Copy).then_inc(wo_hi_done, 1)

            load_kv(0)
            for s in range(WQ_AHEAD):
                load_wq(s, s)
            load_wo(0)
            act.wait_ge(bias_in, 48)
            kv_high(32)
            act.wait_ge(kv_lo_done, 1)
            load_kv(1)

            def evacuate(job, jobs, head, par):
                act.wait_ge(job_done, jobs)
                half = int(job[-1])
                if job[0] == "K":
                    nc.disable_value_cache = True
                    ins = nc.scalar.activation(k_hi[:, par, half * N:(half + 1) * N], M, ACT.Identity,
                                               bias=bk[:, bass.ds(head & (HEADS - 1), 1)])
                    nc.disable_value_cache = False
                elif job in ("V0", "V1"):
                    ins = nc.scalar.activation(v_t[:, half, :], M, ACT.Copy)
                else:
                    ins = nc.scalar.activation(flat(v_hi[:, par, half * QT:(half + 1) * QT, :]), M, ACT.Copy)
                ins.then_inc(job_hi_done, 1)

            def q_split(m, half):
                rows = q_all[:, bass.ds(m, 1), half * 32:half * 32 + 32, :].rearrange("p a r c -> p (a r c)")
                nc.scalar.activation(q_hi[:, half, :], rows, ACT.Copy).then_inc(q_hi_done, 1)

            def wq_high(before, slot, loads, block_):
                act.wait_ge(wq_loaded[slot], loads)
                wait(act, qp_done, before + (1 - LOADS))
                nc.scalar.activation(flat(wq_hi[:, slot, :, :]), flat(wq_in[:, slot, :, :]), ACT.Copy
                                     ).then_inc(wq_hi_done, 1)
                wait(act, wq_lo_done, before)
                load_wq(block_ + WQ_AHEAD, (slot + WQ_AHEAD) % LOADS)

            def group_start(o):
                if isinstance(o, int):
                    for n in range(WQ_AHEAD):
                        wq_high(n, n, 16, n)
                    evacuate("K0", 1, 0, 0)

                def wq_block(before, u):
                    fours = u + WQ_AHEAD >= LOADS
                    wq_high(o * HEADS + (before + (u + WQ_AHEAD)), (u + WQ_AHEAD) % LOADS, (o * HEADS + before) * 4 + 16 * (1 + fours),
                            before + (u + WQ_AHEAD))
                    if isinstance(o, int) and isinstance(before, int):
                        evacuate(FIRST_JOBS[u + 1], u + 2, 0, 0)
                        if FIRST_JOBS[u + 1] == "V1":
                            kv_high(64)
                q_loop(act, wq_block)
                if isinstance(o, int):
                    evacuate("Vt1", 6, 0, 0)
                act.wait_ge(q_done, o * HEADS + HEADS)
                q_split(0, 0)

            def pt_high(b, par, i):
                for ch in range(banks_of(i)):
                    at = chunk_of(i) + ch
                    blocks = min(QT, i + 1 - ch * QT)
                    act.wait_ge(pt_done, b.count(CHUNKS, par * CHUNKS + at + 1))
                    nc.scalar.activation(
                        pt_hi[:, i // 2 % 2, ch * QT:ch * QT + blocks, i % 2 * P:(i % 2 + 1) * P],
                        T[at % 2][:, 0:blocks * P].rearrange("p (a b) -> p a b", b=P), ACT.Copy
                    ).then_inc(pt_hi_done, 1)

            def o_high(b, par, half):
                act.wait_ge(pv_done, b.count(4, par * 4 + 2 * half + 2))
                nc.disable_value_cache = True
                nc.scalar.activation(o_hi[:], O, ACT.Identity, bias=bv[:, bass.ds(b.head(par) & (HEADS - 1), 1)]
                                     ).then_inc(o_hi_done, 1)
                nc.disable_value_cache = False

            def exps(b, t):
                act.wait_ge(max_done, b.count(TILES, t + 1))
                width = (t % TILES + 1) * P
                nc.scalar.activation(probs[:, t % 4, 0:width], flat(S[t % 2])[:, 0:width], ACT.Exp,
                                     bias=neg_max[:, t:t + 1], accum_out=row_sum[:, t:t + 1]
                                     ).then_inc(exp_done, 1)

            def pair(b):
                for t in range(2 * TILES):
                    par, i = divmod(t, TILES)
                    if i - 1 in LATE_AT:
                        evacuate(LATE_AT[i - 1], b.jobs(par, LATE_AT[i - 1]), b.head(par + 1), 1 - par)
                    if lagging(b, t, LAG):
                        pt_high(b, *lagging(b, t, LAG))
                    if FIRST_AT.get(i) in ON_SCALAR:
                        evacuate(FIRST_AT[i], b.jobs(par, FIRST_AT[i]), b.head(par + 1), 1 - par)
                    if i in (0, 4) and not (b.first and par == 0):
                        o_high(b, par - 1, i // 4)
                    if i > 0 and i - 1 not in EAGER:
                        exps(b, t - 1)
                    if EARLY_AT.get(i) in ON_SCALAR:
                        evacuate(EARLY_AT[i], b.jobs(par, EARLY_AT[i]), b.head(par + 1), 1 - par)
                    if i == 1:
                        act.wait_ge(scores_done, b.count(TILES, t))
                        q_split(b.p * 2 + par, 1)
                    if i == 2:
                        wo_high(b.count(16, par * 16 + 16), par)
                    if i == 5:
                        act.wait_ge(scores_done, b.count(TILES, t))
                        q_split((b.p * 2 + (par + 1)) & (GROUP - 1), 0)
                    if i == 6:
                        kv_high(b.count(32, par * 32 + 96))
                    if i in EAGER:
                        exps(b, t)
                    if i == 3:
                        act.wait_ge(kv_lo_done, b.count(1, par + 2))
                        load_kv(b.head(par + 2))
                        act.wait_ge(wo_lo_done, b.count(1, par + 1))
                        load_wo(b.head(par + 1))

            def drain(b):
                o_high(b, -1, 0)
                for i in range(TILES - LAG, TILES):
                    pt_high(b, -1, i)
                o_high(b, -1, 1)
            loops(act, group_start, pair, drain)
            act.wait_ge(kv_loaded, 32 * (BATCH * HEADS + 2))
            act.wait_ge(wo_loaded, 16 * (BATCH * HEADS + 1))
            for s in range(LOADS):
                act.wait_ge(wq_loaded[s], 16 * ((GROUPS * HEADS + 2 * WQ_AHEAD - s + LOADS - 1) // LOADS))

        @block.gpsimd
        def _(pool):
            nc.gpsimd.memset(ident_b[:], 0.0).then_inc(masks_zeroed, 1)
            nc.gpsimd.memset(mask_b[:], 0.0).then_inc(masks_zeroed, 1)
            nc.gpsimd.memset(minus_one[:], -1.0).then_inc(masks_zeroed, 1)
            pool.wait_ge(masks_zeroed, 3)
            nc.gpsimd.affine_select(out=ident_b[:], in_=ident_b[:], compare_op=ALU.not_equal, fill=1.0, base=0,
                                    pattern=[[-1, P]], channel_multiplier=1).then_inc(masks_made, 1)
            nc.gpsimd.affine_select(out=mask_b[:], in_=mask_b[:], compare_op=ALU.is_ge, fill=MASKED, base=0,
                                    pattern=[[-1, P]], channel_multiplier=1).then_inc(masks_made, 1)

            def low(dst, src, high, high_done, count, done):
                pool.wait_ge(high_done, count)
                nc.gpsimd.tensor_tensor(dst, src, high.bitcast(F32), ALU.subtract).then_inc(done, 1)

            def kv_low(count):
                low(flat(kv_lo[:]), flat(kv_in[:]), flat(kv_hi[:]), kv_hi_done, count, kv_lo_done)

            def wo_low(count, slot):
                low(wo_lo[:, slot, :], wo_in[:], wo_hi[:, slot, :], wo_hi_done, count, wo_lo_done)

            def q_low(m, half, count):
                rows = q_all[:, bass.ds(m, 1), half * 32:half * 32 + 32, :].rearrange("p a r c -> p (a r c)")
                low(q_lo[:, half, :], rows, q_hi[:, half, :], q_hi_done, count, q_lo_done)

            kv_low(1)

            def wq_low(block_, slot):
                low(flat(wq_lo[:, slot, :, :]), flat(wq_in[:, slot, :, :]), flat(wq_hi[:, slot, :, :]),
                    wq_hi_done, block_ + 1, wq_lo_done)

            def group_start(o):
                if isinstance(o, int):
                    for n in range(WQ_AHEAD):
                        wq_low(n, n)

                def wq_block(before, u):
                    wq_low(o * HEADS + (before + (u + WQ_AHEAD)), (u + WQ_AHEAD) % LOADS)
                    if isinstance(o, int) and isinstance(before, int) and FIRST_JOBS[u + 1] == "V1":
                        kv_low(2)
                q_loop(pool, wq_block)
                q_low(0, 0, o * SPLITS + 1)

            def pair(b):
                splits = lambda par, half: b.o * SPLITS + b.p * 4 + (2 * par + half + 1)
                for t in range(2 * TILES):
                    par, i = divmod(t, TILES)
                    pool.wait_ge(exp_done, b.count(TILES, t + 1))
                    nc.gpsimd.tensor_tensor(inv_sum[:, t:t + 1], row_sum[:, t:t + 1], minus_one[:], ALU.pow
                                            ).then_inc(inv_done, 1)
                    pool.wait_ge(inv_done, b.count(TILES, t + 1))
                    row = probs[:, t % 4, 0:(i + 1) * P]
                    nc.gpsimd.tensor_tensor(row, row, inv_sum[:, t:t + 1].to_broadcast([P, (i + 1) * P]),
                                            ALU.mult).then_inc(probs_done, 1)
                    if i == 0:
                        q_low(b.p * 2 + par, 1, splits(par, 1))
                    if i == 2:
                        wo_low(b.count(1, par + 1), par)
                    if i == 4:
                        q_low((b.p * 2 + (par + 1)) & (GROUP - 1), 0, splits(par, 2))
                    if i == 5:
                        kv_low(b.count(1, par + 3))
            loops(pool, group_start, pair, lambda b: None)

        @block.vector
        def _(dve):
            dve.wait_ge(bias_in, 48)

            def evacuate(job, jobs, hi, head, par):
                if hi is not None:
                    dve.wait_ge(job_hi_done, hi)
                half = int(job[-1]) if job[0] != "O" else int(job[1])
                if job[0] == "K":
                    cols = slice(half * N, (half + 1) * N)
                    ins = nc.vector.scalar_tensor_tensor(
                        k_lo[:, par, cols], M, bk[:, bass.ds(head & (HEADS - 1), 1)],
                        k_hi[:, par, cols].bitcast(F32), ALU.add, ALU.subtract)
                elif job[0] == "V":
                    blocks = slice(half * QT, (half + 1) * QT)
                    ins = nc.vector.tensor_tensor(flat(v_lo[:, par, blocks, :]), M,
                                                  flat(v_hi[:, par, blocks, :]).bitcast(F32), ALU.subtract)
                else:
                    dve.wait_ge(job_done, jobs)
                    cols = acc[:, "ab".index(job[2]), acc_cols(head, half)]
                    ins = nc.vector.tensor_tensor(cols, M, cols, ALU.add)
                ins.then_inc(job_lo_done, 1)

            def group_start(o):
                wait(dve, q_lo_done, o * SPLITS)
                if isinstance(o, int):
                    evacuate("K0", None, 1, 0, 0)

                def q_block(before, u):
                    dve.wait_ge(qp_done, o * HEADS + (before + (u + 1)))
                    dst = q_all[:].rearrange("p m r c -> p (m r) c")[:, :, bass.ds(before + u, 1)]
                    nc.vector.tensor_scalar(
                        dst.rearrange("p a b -> p (a b)"), S[u % 2][:, 0, :], bq[:, bass.ds(before + u, 1)],
                        SCALE, ALU.add, ALU.mult).then_inc(q_done, 1)
                    if isinstance(o, int) and isinstance(before, int) and FIRST_JOBS[u + 1] in ON_VECTOR:
                        evacuate(FIRST_JOBS[u + 1], None, u + 2, 0, 0)
                q_loop(dve, q_block)
                if isinstance(o, int):
                    evacuate("Vt1", None, 6, 0, 0)

            def pt_low(b, par, i, ch):
                at = chunk_of(i) + ch
                blocks = min(QT, i + 1 - ch * QT)
                dve.wait_ge(pt_hi_done, b.count(CHUNKS, par * CHUNKS + at + 1))
                where = (slice(None), i // 2 % 2, slice(ch * QT, ch * QT + blocks), slice(i % 2 * P, (i % 2 + 1) * P))
                nc.vector.tensor_tensor(pt_lo[where], T[at % 2][:, 0:blocks * P].rearrange("p (a b) -> p a b", b=P),
                                        pt_hi[where].bitcast(F32), ALU.subtract).then_inc(pt_lo_done, 1)

            def o_low(b, par, half):
                dve.wait_ge(o_hi_done, b.count(2, par * 2 + half + 1))
                nc.vector.scalar_tensor_tensor(o_lo[:], O, bv[:, bass.ds(b.head(par) & (HEADS - 1), 1)],
                                               o_hi[:].bitcast(F32), ALU.add, ALU.subtract).then_inc(o_lo_done, 1)

            def pair(b):
                for t in range(2 * TILES):
                    par, i = divmod(t, TILES)
                    follows = not (b.first and par == 0)

                    def take_out(name):
                        if name in ON_VECTOR and name[0] != "O":
                            evacuate(name, None, b.hi(par, name), b.head(par + 1), 1 - par)
                        elif name in ON_VECTOR and follows:
                            evacuate(name, b.jobs(par, name), None, b.head(par - 1), None)

                    between = FIRST_AT.get(i) == "O0a"
                    if lagging(b, t, LAG):
                        tile = lagging(b, t, LAG)
                        pt_low(b, *tile, 0)
                        if between:
                            take_out(FIRST_AT[i])
                        if banks_of(tile[1]) > 1:
                            pt_low(b, *tile, 1)
                    if not between:
                        take_out(FIRST_AT.get(i))
                    if i in (0, 4) and follows:
                        o_low(b, par - 1, i // 4)
                    if i == 4:
                        take_out(LATE_AT[i])
                    hurry = EARLY_AT.get(i) == "O1a"
                    if hurry:
                        take_out(EARLY_AT[i])
                    dve.wait_ge(scores_done, b.count(TILES, t + 1))
                    nc.vector.tensor_reduce(neg_max[:, t:t + 1], flat(S[t % 2])[:, 0:(i + 1) * P], AX.X, ALU.max,
                                            negate=True).then_inc(max_done, 1)
                    if not hurry:
                        take_out(EARLY_AT.get(i))

            def drain(b):
                o_low(b, -1, 0)
                for n, i in enumerate(range(TILES - LAG, TILES)):
                    for ch in range(banks_of(i)):
                        pt_low(b, -1, i, ch)
                    if n < 2:
                        evacuate(OUTPUTS[n], b.jobs(0, OUTPUTS[n]), None, b.head(-1), None)
                o_low(b, -1, 1)
                for job in OUTPUTS[2:]:
                    evacuate(job, b.jobs(0, job), None, b.head(-1), None)
            loops(dve, group_start, pair, drain)

        @block.tensor
        def _(pe):
            pe.wait_ge(masks_made, 2)

            def project(job, head, weights):
                cols = bass.ds(((head >> 4) & (BATCH - 1)) * SEQ + int(job[1]) * N, N)
                part = slice(0, DH) if job[0] == "K" else slice(DH, 2 * DH)
                pe.wait_ge(kv_lo_done, weights)
                for ch in range(KC):
                    last = split_matmul(nc, M, kv_hi[:, ch, part], kv_lo[:, ch, part], xn_hi[:, ch, cols],
                                        xn_lo[:, ch, cols], ch == 0, ch == KC - 1)
                return last

            def v_rows(half):
                for t in range(QT):
                    last = nc.tensor.transpose(M[:, t * P:(t + 1) * P], v_t[:, half, t * P:(t + 1) * P], ident[:])
                return last

            def first_job(n):
                job = FIRST_JOBS[n]
                if n > 0 and FIRST_JOBS[n - 1] in ("V0", "V1"):
                    pe.wait_ge(job_hi_done, n)
                elif n > 0:
                    pe.wait_ge(job_lo_done, sum(other in ON_VECTOR for other in FIRST_JOBS[:n]))
                last = v_rows(int(job[-1])) if job[:2] == "Vt" else project(job, 0, 1)
                last.then_inc(job_done, 1)

            def group_start(o):
                wait(pe, exp_done, o * GROUP * TILES)
                if isinstance(o, int):
                    first_job(0)

                def q_block(before, u):
                    pe.wait_ge(wq_lo_done, o * HEADS + (before + (u + 1)))
                    if not (isinstance(before, int) and u < 2):
                        pe.wait_ge(q_done, o * HEADS + (before + (u - 1)))
                    cols = bass.ds(o * N, N)
                    for ch in range(KC):
                        last = split_matmul(nc, S[u % 2][:, 0, :], wq_hi[:, u, ch, :], wq_lo[:, u, ch, :],
                                            xn_hi[:, ch, cols], xn_lo[:, ch, cols], ch == 0, ch == KC - 1)
                    last.then_inc(qp_done, 1)
                    if isinstance(o, int) and isinstance(before, int):
                        first_job(u + 1)
                q_loop(pe, q_block)
                if isinstance(o, int):
                    first_job(len(FIRST_JOBS) - 1)

            def scores(b, t):
                par, i = divmod(t, TILES)
                if i == 0 and b.first and par == 0:
                    pe.wait_ge(job_lo_done, b.count(len(ON_VECTOR), 4))
                elif i == 0:
                    pe.wait_ge(job_lo_done, b.lo(par - 1, "K1"))
                if i % QT == 0:
                    pe.wait_ge(q_lo_done, b.o * SPLITS + b.p * 4 + (2 * par + i // QT + 1))
                wait(pe, exp_done, b.count(TILES, t - 1))
                half, cols = i // QT, slice(i % QT * P, (i % QT + 1) * P)
                for bank in range(i // QT + 1):
                    width = min(N, (i + 1) * P - bank * N)
                    keys = slice(bank * N, bank * N + width)
                    diagonal = bank == i // QT
                    last = split_matmul(nc, S[t % 2][:, bank, 0:width], q_hi[:, half, cols], q_lo[:, half, cols],
                                        k_hi[:, par, keys], k_lo[:, par, keys], True, not diagonal)
                    if diagonal:
                        last = nc.tensor.matmul(S[t % 2][:, bank, cols], ident_b[:], mask_b[:], start=False, stop=True)
                last.then_inc(scores_done, 1)

            def transposes(b, par, i, slot):
                pe.wait_ge(probs_done, b.count(TILES, par * TILES + i + 1))
                for ch in range(banks_of(i)):
                    at = chunk_of(i) + ch
                    wait(pe, pt_lo_done, b.count(CHUNKS, par * CHUNKS + at - 1))
                    for n in range(min(QT, i + 1 - ch * QT)):
                        s = ch * QT + n
                        last = nc.tensor.transpose(T[at % 2][:, n * P:(n + 1) * P], probs[:, slot, s * P:(s + 1) * P],
                                                   ident[:])
                    last.then_inc(pt_done, 1)

            def with_v(b, par, q):
                pe.wait_ge(pt_lo_done, b.count(CHUNKS, par * CHUNKS + chunk_of(2 * q + 1) + banks_of(2 * q + 1)))
                if q % 2 == 0:
                    wait(pe, o_lo_done, b.count(2, par * 2 + q // 2))
                for s in range(2 * q + 2):
                    first = P if s == 2 * q + 1 else 0
                    out = O[:, q % 2 * QUARTER + first:(q % 2 + 1) * QUARTER]
                    last = split_matmul(nc, out, v_hi[:, par % 2, s, :], v_lo[:, par % 2, s, :],
                                        pt_hi[:, q % 2, s, first:], pt_lo[:, q % 2, s, first:], s == 0, s == 2 * q + 1)
                last.then_inc(pv_done, 1)

            def output(b, par, half, h):
                pe.wait_ge(o_lo_done, b.count(2, par * 2 + half + 1))
                cols = slice(h * P, (h + 1) * P)
                return split_matmul(nc, M, wo_hi[:, par % 2, cols], wo_lo[:, par % 2, cols], o_hi[:], o_lo[:], True, True)

            def job(b, par, name):
                if name is None or (b.first and par == 0 and name in OUTPUTS):
                    return
                before = [other for other in JOBS[:JOBS.index(name)]
                          if not (b.first and par == 0 and other[0] == "O")]
                if isinstance(b, Drain) or not before:
                    pe.wait_ge(job_lo_done, b.lo(par, name, before=1))
                elif before[-1] in ("V0", "V1"):
                    pe.wait_ge(job_hi_done, b.hi(par, before[-1]))
                else:
                    pe.wait_ge(job_lo_done, b.lo(par, before[-1]))
                if name in ("K0", "K1", "V0", "V1"):
                    last = project(name, b.head(par + 1), b.count(1, par + 2))
                elif name in ("Vt0", "Vt1"):
                    last = v_rows(int(name[-1]))
                else:
                    if name == "O0a":
                        pe.wait_ge(wo_lo_done, b.count(1, par))
                    last = output(b, par - 1, int(name[1]), "ab".index(name[2]))
                last.then_inc(job_done, 1)

            def pair(b):
                for t in range(2 * TILES):
                    par, i = divmod(t, TILES)
                    if lagging(b, t, LAG):
                        transposes(b, *lagging(b, t, LAG), (t - LAG) % 4)
                    job(b, par, FIRST_AT.get(i))
                    scores(b, t)
                    job(b, par, EARLY_AT.get(i))
                    if t % 2 == 1 and lagging(b, t, LAG + 2):
                        at = lagging(b, t, LAG + 2)
                        with_v(b, at[0], at[1] // 2)
                    job(b, par, LATE_AT.get(i))

            def drain(b):
                transposes(b, -1, 5, 5 % 4)
                job(b, 0, "O0a")
                transposes(b, -1, 6, 6 % 4)
                job(b, 0, "O0b")
                with_v(b, -1, 2)
                transposes(b, -1, 7, 7 % 4)
                with_v(b, -1, 3)
                job(b, 0, "O1a")
                job(b, 0, "O1b")
            loops(pe, group_start, pair, drain)


def finish(nc, sh, d, out):
    ps, acc, ident = sh["ps"], sh["acc"], sh["ident"]
    PAIRS = NT // 2
    with ExitStack() as c:
        sem = lambda name: c.enter_context(nc.semaphore(name))
        x_res = c.enter_context(nc.sbuf_tensor("x_res", [P, NT, DM], F32))
        x_res_in = sem("x_res_in")
        out_t_done, out_added, out_stored = sem("out_t_done"), sem("out_added"), sem("out_stored")
        block = c.enter_context(nc.Block())
        rows = lambda dram: dram.rearrange("(t p) k -> p t k", p=P)

        @block.sync
        def _(sp):
            sp.dma_start(x_res[:], rows(d["x"])).then_inc(x_res_in, 16)
            for g in range(PAIRS):
                sp.wait_ge(out_added, g + 1)
                sp.dma_start(rows(out)[:, 2 * g:2 * g + 2, :], x_res[:, 2 * g:2 * g + 2, :]
                             ).then_inc(out_stored, 16)
            sp.wait_ge(out_stored, 16 * PAIRS)

        @block.tensor
        def _(pe):
            for g in range(PAIRS):
                for t in range(2):
                    for h in range(KC):
                        last = nc.tensor.transpose(ps[:, g, (2 * t + h) * P:(2 * t + h + 1) * P],
                                                   acc[:, h, (2 * g + t) * P:(2 * g + t + 1) * P], ident[:])
                last.then_inc(out_t_done, 1)

        @block.vector
        def _(dve):
            dve.wait_ge(x_res_in, 16)
            for g in range(PAIRS):
                dve.wait_ge(out_t_done, g + 1)
                res = flat(x_res[:, 2 * g:2 * g + 2, :])
                nc.vector.tensor_tensor(res, ps[:, g, :], res, ALU.add).then_inc(out_added, 1)


def layer(nc, d, out):
    with ExitStack() as c:
        sb = lambda name, shape, dt: c.enter_context(nc.sbuf_tensor(name, shape, dt))
        sh = {
            "xn_hi": sb("xn_hi", [P, KC, TOK], F32R), "xn_lo": sb("xn_lo", [P, KC, TOK], F32R),
            "acc": sb("acc", [P, KC, TOK], F32), "ident": sb("ident", [P, P], F32),
            "ps": c.enter_context(nc.psum_tensor("ps", [P, 8, N], F32)),
        }
        norm_and_ffn(nc, sh, d)
        attention(nc, sh, d)
        finish(nc, sh, d, out)


def kernel(**inputs):
    import concourse.bacc as bacc
    from concourse.bass_utils import run_bass_kernel_spmd

    names = {
        "x": ("L0_attn_x", (TOK, DM)), "wq": ("L0_attn_Wq", None), "bq": ("L0_attn_bq", None),
        "wk": ("L0_attn_Wk", None), "bk": ("L0_attn_bk", None), "wv": ("L0_attn_Wv", None),
        "bv": ("L0_attn_bv", None), "wo": ("L0_attn_Wo", None), "bo": ("L0_attn_bo", None),
        "gate": ("L0_ffn_gate_W_packed", None), "gate_scales": ("L0_ffn_gate_scales", None),
        "up": ("L0_ffn_up_W_packed", None), "up_scales": ("L0_ffn_up_scales", None),
        "down": ("L0_ffn_down_W_packed", None), "down_scales": ("L0_ffn_down_scales", None),
    }
    nc = bacc.Bacc("TRN2", target_bir_lowering=False, num_devices=1)
    arrays, d = {}, {}
    for short, (name, shape) in names.items():
        a = np.ascontiguousarray(inputs[name])
        if shape is not None:
            a = a.reshape(shape)
        elif a.ndim == 1:
            a = np.ascontiguousarray(a.reshape(-1, P).T)
        arrays[f"in_{short}"] = a
        d[short] = nc.dram_tensor(f"in_{short}", a.shape, mybir.dt.from_np(a.dtype), kind="ExternalInput").ap()
    out = nc.dram_tensor("out", (TOK, DM), F32, kind="ExternalOutput").ap()
    layer(nc, d, out)
    result = run_bass_kernel_spmd(nc, [arrays], core_ids=[0])
    return np.asarray(result.results[0]["out"]).reshape(BATCH, SEQ, DM)
```

```python
from contextlib import ExitStack

import numpy as np
import concourse.bass as bass
from concourse import mybir

F32, F32R = mybir.dt.float32, mybir.dt.float32r
BF16, I32 = mybir.dt.bfloat16, mybir.dt.int32
ACT = mybir.ActivationFunctionType
ALU = mybir.AluOpType
AX = mybir.AxisListType

P = 128
BATCH, SEQ, DM = 2, 1024, 256
TOK = BATCH * SEQ
HEADS, DH = 16, 128
FF = 2048
QBLOCK = 32
KC = DM // P
NT = TOK // P
N = 512
EPS = 1e-5
SCALE = float(np.float32(1.0) / np.sqrt(np.float32(DH)))
GELU_A, GELU_B = 0.7978845608028654, 0.044715
LOADS = 4
WQ_AHEAD = 3
MASKED = -3.0e38


def flat(ap):
    return ap.rearrange("p a b -> p (a b)")


def split_matmul(nc, out, w_hi, w_lo, m_hi, m_lo, start, stop):
    nc.tensor.matmul(out, w_hi, m_hi, start=start, stop=False)
    nc.tensor.matmul(out, w_hi, m_lo, start=False, stop=False)
    return nc.tensor.matmul(out, w_lo, m_hi, start=False, stop=stop)


def wait(eng, sem, count):
    if isinstance(count, int) and count <= 0:
        return
    eng.wait_ge(sem, count)


def load_kv(eng, sh, d, head):
    cols = bass.ds((head & (HEADS - 1)) * DH, DH)
    for part, name in enumerate(("wk", "wv")):
        eng.dma_start(sh["kv_in"][:, :, part * DH:(part + 1) * DH],
                      d[name].rearrange("(c p) n -> p c n", p=P)[:, :, cols]).then_inc(sh["kv_loaded"], 16)


def load_wq(eng, sh, d, block_, slot):
    eng.dma_start(sh["wq_in"][:, slot, :, :], d["wq"].rearrange("(c p) n -> p c n", p=P)[
        :, :, bass.ds((block_ & (HEADS - 1)) * DH, DH)]).then_inc(sh["wq_loaded"][slot], 16)


def kv_high(nc, act, sh, loaded):
    act.wait_ge(sh["kv_loaded"], loaded)
    nc.scalar.activation(flat(sh["kv_hi"][:]), flat(sh["kv_in"][:]), ACT.Copy).then_inc(sh["kv_hi_done"], 1)


def kv_low(nc, pool, sh, count):
    pool.wait_ge(sh["kv_hi_done"], count)
    nc.gpsimd.tensor_tensor(flat(sh["kv_lo"][:]), flat(sh["kv_in"][:]), flat(sh["kv_hi"][:]).bitcast(F32),
                            ALU.subtract).then_inc(sh["kv_lo_done"], 1)


def norm_and_ffn(nc, sh, d):
    NJ = FF // P
    TC = TOK // N
    BODY = 4 * TC
    GROUPS = BODY // 2
    W6 = 6 * P
    ps, acc, ident = sh["ps"], sh["acc"], sh["ident"]
    xn_hi, xn_lo = sh["xn_hi"], sh["xn_lo"]
    G = [ps[:, i, :] for i in (0, 1)]
    U = [ps[:, i, :] for i in (2, 3)]
    D = ps[:, 4:6, :]
    WT = ps[:, 6:8, :]

    with ExitStack() as c:
        sb = lambda name, shape, dt: c.enter_context(nc.sbuf_tensor(name, shape, dt))
        sem = lambda name: c.enter_context(nc.semaphore(name))
        x_all = sb("x_all", [P, NT, DM], F32)
        stats = sb("stats", [P, NT, 6], F32)
        mean_var = sb("mean_var", [P, NT, 2], F32)
        minus_half = sb("minus_half", [P, NT], F32)
        var_eps = sb("var_eps", [P, NT], F32)
        rstd = sb("rstd", [P, NT], F32)
        xn_rows = sb("xn_rows", [P, 2, 4, DM], F32)
        bo_col = sb("bo_col", [P, KC], F32)
        raw = sb("raw", [P, 2, W6 // 2], I32)
        scales = sb("scales", [P, NJ, W6 // QBLOCK], F32)
        mag = sb("mag", [P, W6], I32)
        sgn = sb("sgn", [P, W6], I32)
        mag_f = sb("mag_f", [P, W6], F32)
        over4 = sb("over4", [P, W6], F32)
        over6 = sb("over6", [P, W6], F32)
        half_sign = sb("half_sign", [P, W6], F32)
        vals = sb("vals", [P, W6], F32)
        w_rows = sb("w_rows", [P, W6], F32)
        offsets = sb("offsets", [P, 3], F32)
        w_hi = sb("w_hi", [P, 4, 6, P], F32R)
        w_lo = sb("w_lo", [P, 4, 6, P], F32R)
        sq = sb("sq", [P, 2, N], F32)
        inner = sb("inner", [P, 2, N], F32)
        th = sb("th", [P, 2, N], F32)
        gated = sb("gated", [P, 2, N], F32)
        hid = sb("hid", [P, 4, N], F32)
        hid_hi = sb("hid_hi", [P, 4, N], F32R)
        hid_lo = sb("hid_lo", [P, 4, N], F32R)

        x_in = [sem(f"x_in{q}") for q in range(4)]
        raw_in = [sem(f"raw_in{s}") for s in range(2)]
        scales_in, bo_in = sem("scales_in"), sem("bo_in")
        offsets_set, stats_done, mean_done, eps_done, rstd_done, rows_done = (
            sem(s) for s in ("offsets_set", "stats_done", "mean_done", "eps_done", "rstd_done", "rows_done"))
        xt_done, xt_hi_done, xt_lo_done = sem("xt_done"), sem("xt_hi_done"), sem("xt_lo_done")
        ints_done, linear_done, vals_done, w_rows_done = (
            sem(s) for s in ("ints_done", "linear_done", "vals_done", "w_rows_done"))
        wt_done, wt_hi_done, wt_lo_done = sem("wt_done"), sem("wt_hi_done"), sem("wt_lo_done")
        gu_done, sq_done, inner_done, th_done, gated_done, hid_done = (
            sem(s) for s in ("gu_done", "sq_done", "inner_done", "th_done", "gated_done", "hid_done"))
        hid_hi_done, hid_lo_done, down_done, acc_done = (
            sem(s) for s in ("hid_hi_done", "hid_lo_done", "down_done", "acc_done"))
        zeroed, made = sem("ident_zeroed"), sem("ident_made")
        block = c.enter_context(nc.Block())

        def xt_bank(b):
            return b if b < 4 else 4 + b % KC

        def load_raw(eng, j, slot):
            wait(eng, ints_done, j - 1)
            if isinstance(j, int):
                j = j % NJ
            row, col = j * P, j * (P // 2)
            dst = raw[:, slot, :]
            eng.dma_start(dst[:, 0:P], d["gate"][bass.ds(row, P), :]).then_inc(raw_in[slot], 16)
            eng.dma_start(dst[:, P:2 * P], d["up"][bass.ds(row, P), :]).then_inc(raw_in[slot], 16)
            eng.dma_start(dst[:, 2 * P:3 * P].rearrange("p (c k) -> p c k", c=2),
                          d["down"].rearrange("(c p) k -> p c k", p=P)[:, :, bass.ds(col, P // 2)]
                          ).then_inc(raw_in[slot], 16)

        def load_x(eng, g):
            tiles = slice(4 * g, 4 * g + 4)
            eng.dma_start(x_all[:, tiles, :], d["x"].rearrange("(t p) k -> p t k", p=P)[:, tiles, :]
                          ).then_inc(x_in[g], 16)

        @block.sync
        def _(sp):
            load_raw(sp, 0, 0)
            load_x(sp, 1)
            load_x(sp, 3)
            for dst, name in ((scales[:, :, 0:8], "gate_scales"), (scales[:, :, 8:16], "up_scales")):
                sp.dma_start(dst, d[name].rearrange("(j p) b -> p j b", p=P)).then_inc(scales_in, 16)
            for h in range(KC):
                sp.dma_start(scales[:, :, 16 + 4 * h:20 + 4 * h],
                             d["down_scales"][h * P:(h + 1) * P, :].rearrange("p (j b) -> p j b", b=4)
                             ).then_inc(scales_in, 16)
            sp.dma_start(bo_col[:], d["bo"]).then_inc(bo_in, 16)
            load_raw(sp, 2, 0)

            def body(it):
                for m in range(4):
                    load_raw(sp, it * 4 + (3 + m), (3 + m) % 2)
            body(0)
            with sp.Fori(1, NJ // 4 - 1) as it:
                body(it)
            body(NJ // 4 - 1)
            load_kv(sp, sh, d, 0)
            for s in range(WQ_AHEAD):
                load_wq(sp, sh, d, s, s)
            for name in ("bq", "bk", "bv"):
                sp.dma_start(sh[name][:], d[name]).then_inc(sh["bias_in"], 16)

        @block.gpsimd
        def _(pool):
            nc.gpsimd.memset(ident[:], 0.0).then_inc(zeroed, 1)
            nc.gpsimd.memset(minus_half[:], -0.5).then_inc(offsets_set, 1)
            nc.gpsimd.memset(offsets[:, 0:1], -4.0).then_inc(offsets_set, 1)
            nc.gpsimd.memset(offsets[:, 1:2], -12.0).then_inc(offsets_set, 1)
            nc.gpsimd.memset(offsets[:, 2:3], 0.5).then_inc(offsets_set, 1)
            pool.wait_ge(zeroed, 1)
            nc.gpsimd.affine_select(out=ident[:], in_=ident[:], compare_op=ALU.not_equal, fill=1.0, base=0,
                                    pattern=[[-1, P]], channel_multiplier=1).then_inc(made, 1)
            for dst, value in ((sh["ident_b"], 0.0), (sh["mask_b"], 0.0), (sh["minus_one"], -1.0)):
                nc.gpsimd.memset(dst[:], value).then_inc(sh["masks_zeroed"], 1)
            pool.wait_ge(sh["masks_zeroed"], 3)
            for dst, op, fill in ((sh["ident_b"], ALU.not_equal, 1.0), (sh["mask_b"], ALU.is_ge, MASKED)):
                nc.gpsimd.affine_select(out=dst[:], in_=dst[:], compare_op=op, fill=fill, base=0,
                                        pattern=[[-1, P]], channel_multiplier=1).then_inc(sh["masks_made"], 1)

            def piece(j, part):
                if part == 0:
                    pool.wait_ge(linear_done, j * 4 + 2)
                    wait(pool, w_rows_done, j)
                    nc.gpsimd.tensor_tensor(vals[:], over4[:], over6[:], ALU.add).then_inc(vals_done, 1)
                elif part == 1:
                    pool.wait_ge(linear_done, j * 4 + 3)
                    pool.wait_ge(vals_done, j * 3 + 1)
                    nc.gpsimd.tensor_tensor(vals[:], vals[:], mag_f[:], ALU.add).then_inc(vals_done, 1)
                elif part == 2:
                    pool.wait_ge(linear_done, j * 4 + 4)
                    pool.wait_ge(vals_done, j * 3 + 2)
                    nc.gpsimd.tensor_tensor(vals[:], vals[:], half_sign[:], ALU.mult).then_inc(vals_done, 1)
                else:
                    pool.wait_ge(vals_done, j * 3 + 3)
                    wait(pool, wt_done, j)
                    scale = scales[:, bass.ds(j & (NJ - 1), 1), :].rearrange("p a b -> p b a")
                    nc.gpsimd.tensor_tensor(
                        w_rows[:].rearrange("p (b k) -> p b k", k=QBLOCK),
                        vals[:].rearrange("p (b k) -> p b k", k=QBLOCK),
                        scale.to_broadcast([P, W6 // QBLOCK, QBLOCK]),
                        ALU.mult).then_inc(w_rows_done, 1)

            def rstds(g):
                pool.wait_ge(eps_done, g + 1)
                tiles = slice(4 * g, 4 * g + 4)
                nc.gpsimd.tensor_tensor(rstd[:, tiles], var_eps[:, tiles], minus_half[:, tiles], ALU.pow
                                        ).then_inc(rstd_done, 1)

            pool.wait_ge(offsets_set, 4)
            rstds(0)
            rstds(1)
            for part in range(4):
                if part == 3:
                    pool.wait_ge(scales_in, 64)
                piece(0, part)
            rstds(2)
            for part in range(4):
                if part == 3:
                    rstds(3)
                piece(1, part)
            for part in range(2):
                piece(2, part)

            def body(it):
                for kk in range(BODY):
                    piece(it * 4 + (2 + (kk + 2) // 4), (kk + 2) % 4)
                    pool.wait_ge(hid_hi_done, it * BODY + (kk + 1))
                    nc.gpsimd.tensor_tensor(hid_lo[:, kk % 4, :], hid[:, kk % 4, :],
                                            hid_hi[:, kk % 4, :].bitcast(F32), ALU.subtract
                                            ).then_inc(hid_lo_done, 1)
            body(0)
            with pool.Fori(1, NJ // 4) as it:
                body(it)
            kv_low(nc, pool, sh, 1)

        @block.scalar
        def _(act):
            load_x(act, 0)
            load_raw(act, 1, 1)
            load_x(act, 2)

            def linear(j, parts):
                for part in parts:
                    if part == 0:
                        act.wait_ge(ints_done, j + 1)
                    wait(act, vals_done, j * 3 - (2, 2, 1, 0)[part])
                    if part == 0:
                        ins = nc.scalar.activation(over4[:], mag[:], ACT.Relu, bias=offsets[:, 0:1])
                    elif part == 1:
                        ins = nc.scalar.activation(over6[:], mag[:], ACT.Relu, bias=offsets[:, 1:2], scale=2.0)
                    elif part == 2:
                        ins = nc.scalar.activation(mag_f[:], mag[:], ACT.Copy)
                    else:
                        ins = nc.scalar.activation(half_sign[:], sgn[:], ACT.Identity, bias=offsets[:, 2:3],
                                                   scale=-0.125)
                    ins.then_inc(linear_done, 1)

            def weights_high(j, slot, downs):
                act.wait_ge(wt_done, j + 1)
                wait(act, down_done, downs)
                nc.scalar.activation(w_hi[:, slot, :, :].rearrange("p a b -> p (a b)"), flat(WT)[:, 0:W6],
                                     ACT.Copy).then_inc(wt_hi_done, 1)

            act.wait_ge(offsets_set, 4)
            linear(0, range(4))
            def xn_high(g):
                for b in (2 * g, 2 * g + 1):
                    act.wait_ge(xt_done, b + 1)
                    nc.scalar.activation(xn_hi[:, b % KC, g * N:(g + 1) * N], ps[:, xt_bank(b), :], ACT.Copy
                                         ).then_inc(xt_hi_done, 1)

            xn_high(0)
            xn_high(1)
            linear(1, range(4))
            weights_high(0, 0, 0)
            linear(2, (0, 1))
            weights_high(1, 1, 0)
            xn_high(2)
            linear(2, (2, 3))

            def hid_high(it, kk):
                act.wait_ge(hid_done, it * BODY + (kk + 1))
                wait(act, down_done, it * GROUPS + (kk // 2 - 1))
                nc.scalar.activation(hid_hi[:, kk % 4, :], hid[:, kk % 4, :], ACT.Copy
                                     ).then_inc(hid_hi_done, 1)

            def body(it, first):
                for kk in range(BODY):
                    k1 = it * BODY + (kk + 1)
                    act.wait_ge(gu_done, k1)
                    nc.scalar.activation(sq[:, kk % 2, :], G[kk % 2], ACT.Square, scale=float(np.sqrt(GELU_B))
                                         ).then_inc(sq_done, 1)
                    if not (first and kk == 0):
                        hid_high(it, kk - 1)
                    m = kk // 4
                    linear(it * 4 + (3 + m), ((), (0, 1), (2,), (3,))[kk % 4])
                    act.wait_ge(inner_done, k1)
                    nc.scalar.activation(th[:, kk % 2, :], inner[:, kk % 2, :], ACT.Tanh, scale=GELU_A
                                         ).then_inc(th_done, 1)
                    if first and kk == 0:
                        xn_high(3)
                    if kk % 4 == 3:
                        weights_high(it * 4 + (2 + m), (2 + m) % 4, it * GROUPS + TC * (m // 2))
            body(0, True)
            with act.Fori(1, NJ // 4) as it:
                body(it, False)
            hid_high(NJ // 4 - 1, BODY - 1)
            kv_high(nc, act, sh, 32)

        @block.vector
        def _(dve):
            def integers(j, slot):
                dve.wait_ge(raw_in[slot], (j >> 1) * 48 + 48)
                wait(dve, linear_done, j * 4)
                for dst, mask in ((mag, 7), (sgn, 8)):
                    pairs = dst[:].rearrange("p (k two) -> p k two", two=2)
                    nc.vector.tensor_scalar(pairs[:, :, 0], raw[:, slot, :], mask, None, ALU.bitwise_and)
                    last = nc.vector.tensor_scalar(pairs[:, :, 1], raw[:, slot, :], 4, mask,
                                                   ALU.logical_shift_right, ALU.bitwise_and)
                last.then_inc(ints_done, 1)

            def weights_low(j, slot):
                dve.wait_ge(wt_hi_done, j + 1)
                nc.vector.tensor_tensor(w_lo[:, slot, :, :].rearrange("p a b -> p (a b)"), flat(WT)[:, 0:W6],
                                        w_hi[:, slot, :, :].rearrange("p a b -> p (a b)").bitcast(F32),
                                        ALU.subtract).then_inc(wt_lo_done, 1)

            def statistics(g):
                tiles = range(4 * g, 4 * g + 4)
                dve.wait_ge(x_in[g], 16)
                for t in tiles:
                    nc.vector.bn_stats(stats[:, t, :], x_all[:, t, :]).then_inc(stats_done, 1)
                for t in tiles:
                    dve.wait_ge(stats_done, t + 1)
                    nc.vector.bn_aggr(mean_var[:, t, :], stats[:, t, :]).then_inc(mean_done, 1)
                dve.wait_ge(mean_done, 4 * g + 4)
                nc.vector.tensor_scalar(var_eps[:, 4 * g:4 * g + 4], mean_var[:, 4 * g:4 * g + 4, 1], EPS, None,
                                        ALU.add).then_inc(eps_done, 1)

            def rows(g):
                dve.wait_ge(rstd_done, g + 1)
                wait(dve, xt_done, KC * (g - 1))
                for t in range(4 * g, 4 * g + 4):
                    nc.vector.tensor_scalar(xn_rows[:, g % 2, t % 4, :], x_all[:, t, :], mean_var[:, t, 0:1],
                                            rstd[:, t:t + 1], ALU.subtract, ALU.mult).then_inc(rows_done, 1)

            def xn_low(g):
                for b in (2 * g, 2 * g + 1):
                    ch = b % KC
                    dve.wait_ge(xt_hi_done, b + 1)
                    nc.vector.tensor_tensor(xn_lo[:, ch, g * N:(g + 1) * N], ps[:, xt_bank(b), :],
                                            xn_hi[:, ch, g * N:(g + 1) * N].bitcast(F32), ALU.subtract
                                            ).then_inc(xt_lo_done, 1)

            statistics(0)
            integers(0, 0)
            statistics(1)
            rows(0)
            rows(1)
            integers(1, 1)
            xn_low(0)
            xn_low(1)
            statistics(2)
            weights_low(0, 0)
            rows(2)
            integers(2, 0)
            statistics(3)
            rows(3)
            weights_low(1, 1)
            xn_low(2)
            dve.wait_ge(bo_in, 16)

            def add_down(tc, count, fresh):
                dve.wait_ge(down_done, count)
                cols = slice(tc * N, (tc + 1) * N)
                if fresh:
                    for h in range(KC):
                        last = nc.vector.tensor_scalar(acc[:, h, cols], D[:, h, :], bo_col[:, h:h + 1], None,
                                                       ALU.add)
                else:
                    last = nc.vector.tensor_tensor(acc[:, :, cols], D, acc[:, :, cols], ALU.add)
                last.then_inc(acc_done, 1)

            def body(it, first):
                for kk in range(BODY):
                    s, k1 = kk % 2, it * BODY + (kk + 1)
                    dve.wait_ge(sq_done, k1)
                    nc.vector.scalar_tensor_tensor(inner[:, s, :], sq[:, s, :], 1.0, G[s], ALU.add, ALU.mult
                                                   ).then_inc(inner_done, 1)
                    if kk % 2 == 1 and not (first and kk == 1):
                        add_down((kk - 3) // 2 % TC, it * GROUPS + (kk - 1) // 2, first and kk < 2 * TC + 3)
                    if kk % 4 == 0:
                        integers(it * 4 + (3 + kk // 4), (3 + kk // 4) % 2)
                    dve.wait_ge(th_done, k1)
                    nc.vector.scalar_tensor_tensor(gated[:, s, :], th[:, s, :], 1.0, G[s], ALU.add, ALU.mult
                                                   ).then_inc(gated_done, 1)
                    dve.wait_ge(gated_done, k1)
                    wait(dve, hid_lo_done, it * BODY + (kk - 3))
                    nc.vector.scalar_tensor_tensor(hid[:, kk % 4, :], gated[:, s, :], 0.5, U[s], ALU.mult,
                                                   ALU.mult).then_inc(hid_done, 1)
                    if first and kk == 0:
                        xn_low(3)
                    if kk % 4 == 3:
                        weights_low(it * 4 + (2 + kk // 4), (2 + kk // 4) % 4)
            body(0, True)
            with dve.Fori(1, NJ // 4) as it:
                body(it, False)
            add_down(TC - 1, NJ // 4 * GROUPS, False)

        @block.tensor
        def _(pe):
            pe.wait_ge(made, 1)
            def transpose_xn(g):
                pe.wait_ge(rows_done, 4 * g + 4)
                wait(pe, xt_lo_done, KC * (g - 2) if g < 3 else KC * g)
                for b in (2 * g, 2 * g + 1):
                    for t in range(4):
                        ch = b % KC
                        last = nc.tensor.transpose(ps[:, xt_bank(b), t * P:(t + 1) * P],
                                                   xn_rows[:, g % 2, t, ch * P:(ch + 1) * P], ident[:])
                    last.then_inc(xt_done, 1)

            def transpose_weights(j):
                pe.wait_ge(w_rows_done, j + 1)
                wait(pe, wt_lo_done, j)
                for b in range(6):
                    last = nc.tensor.transpose(WT[:, b // 4, b % 4 * P:(b % 4 + 1) * P],
                                               w_rows[:, b * P:(b + 1) * P], ident[:])
                last.then_inc(wt_done, 1)

            def gate_up(kk, k, slot, new_chunk):
                s, cols = kk % 2, slice(kk // 2 % TC * N, (kk // 2 % TC + 1) * N)
                if new_chunk is not None:
                    pe.wait_ge(wt_lo_done, new_chunk + 1)
                wait(pe, hid_done, k - 1)
                for bank, first_block in ((G[s], 0), (U[s], 2)):
                    for ch in range(KC):
                        last = split_matmul(nc, bank, w_hi[:, slot, first_block + ch, :],
                                            w_lo[:, slot, first_block + ch, :], xn_hi[:, ch, cols],
                                            xn_lo[:, ch, cols], ch == 0, ch == KC - 1)
                last.then_inc(gu_done, 1)

            def down(kk, k, slot):
                pe.wait_ge(hid_lo_done, k + 1)
                if kk % 2 == 0:
                    wait(pe, acc_done, k // 2 if isinstance(k, int) else k >> 1)
                for h in range(KC):
                    last = split_matmul(nc, D[:, h, :], w_hi[:, slot, 4 + h, :], w_lo[:, slot, 4 + h, :],
                                        hid_hi[:, kk % 4, :], hid_lo[:, kk % 4, :], kk % 2 == 0, kk % 2 == 1)
                if kk % 2 == 1:
                    last.then_inc(down_done, 1)

            slot_of = lambda kk: kk // (2 * TC) % 2 * 2 + kk % 2
            transpose_xn(0)
            transpose_xn(1)
            transpose_weights(0)
            pe.wait_ge(xt_lo_done, 2 * KC)

            def body(it, first):
                for kk in range(BODY):
                    k = it * BODY + kk
                    fresh = kk // 2 % TC == 0
                    gate_up(kk, k, slot_of(kk), it * 4 + slot_of(kk) if fresh else None)
                    if first and kk == 0:
                        transpose_weights(1)
                        transpose_xn(2)
                    if first and kk == 1:
                        transpose_xn(3)
                    if first and kk == 2:
                        pe.wait_ge(xt_lo_done, 4 * KC)
                    if not (first and kk < 2):
                        down((kk - 2) % BODY, it * BODY + (kk - 2), slot_of((kk - 2) % BODY))
                    if kk % 4 == 2:
                        transpose_weights(it * 4 + (2 + kk // 4))
            body(0, True)
            with pe.Fori(1, NJ // 4) as it:
                body(it, False)
            for kk in (BODY - 2, BODY - 1):
                down(kk, (NJ // 4 - 1) * BODY + kk, slot_of(kk))


def attention(nc, sh, d, out):
    GROUP = N // (SEQ // HEADS)
    GROUPS = BATCH * HEADS // GROUP
    PAIRS = GROUP // 2
    TILES = SEQ // P
    CHUNKS = 12
    QT = N // P
    QUARTER = 2 * P
    SPLITS = 2 * GROUP + 1
    LAG = 3
    ps, acc, ident = sh["ps"], sh["acc"], sh["ident"]
    xn_hi, xn_lo = sh["xn_hi"], sh["xn_lo"]
    S = [ps[:, 0:2, :], ps[:, 2:4, :]]
    O, M = ps[:, 4, :], ps[:, 5, :]
    T = [ps[:, 6, :], ps[:, 7, :]]

    with ExitStack() as c:
        sb = lambda name, shape, dt: c.enter_context(nc.sbuf_tensor(name, shape, dt))
        sem = lambda name: c.enter_context(nc.semaphore(name))
        ident_b, mask_b, minus_one = sh["ident_b"], sh["mask_b"], sh["minus_one"]
        bk_now, bv_now = sb("bk_now", [P, 2], F32), sb("bv_now", [P, 2], F32)
        bq, bk, bv, wq_in, kv_hi, kv_lo = (sh[name] for name in ("bq", "bk", "bv", "wq_in", "kv_hi", "kv_lo"))
        wo_in = sb("wo_in", [P, DM], F32)
        wo_hi, wo_lo = sb("wo_hi", [P, 2, DM], F32R), sb("wo_lo", [P, 2, DM], F32R)
        wq_hi, wq_lo = sb("wq_hi", [P, LOADS, KC, DH], F32R), sb("wq_lo", [P, LOADS, KC, DH], F32R)
        q_all = sb("q_all", [P, GROUP, SEQ // HEADS, HEADS], F32)
        q_hi, q_lo = sb("q_hi", [P, 2, N], F32R), sb("q_lo", [P, 2, N], F32R)
        k_hi, k_lo = sb("k_hi", [P, 2, SEQ], F32R), sb("k_lo", [P, 2, SEQ], F32R)
        v_hi, v_lo = (sb(name, [P, 2, TILES, DH], F32R) for name in ("v_hi", "v_lo"))
        v_t = sb("v_t", [P, 2, N], F32)
        probs = sb("probs", [P, 4, SEQ], F32)
        neg_max, row_sum, inv_sum = (sb(name, [P, 2 * TILES], F32) for name in ("neg_max", "row_sum", "inv_sum"))
        pt_hi, pt_lo = (sb(name, [P, 2, TILES, QUARTER], F32R) for name in ("pt_hi", "pt_lo"))
        o_hi, o_lo = sb("o_hi", [P, N], F32R), sb("o_lo", [P, N], F32R)

        wo_loaded = sem("wo_loaded")
        bias_in, kv_loaded, wq_loaded, kv_lo_done = (
            sh[name] for name in ("bias_in", "kv_loaded", "wq_loaded", "kv_lo_done"))
        bias_set = sem("bias_set")
        wq_hi_done, wq_lo_done, qp_done, q_done = (sem(s) for s in ("wq_hi_done", "wq_lo_done", "qp_done", "q_done"))
        wo_hi_done, wo_lo_done = sem("wo_hi_done"), sem("wo_lo_done")
        q_hi_done, q_lo_done = sem("q_hi_done"), sem("q_lo_done")
        scores_done, max_done, exp_done, inv_done, probs_done = (
            sem(s) for s in ("scores_done", "max_done", "exp_done", "inv_done", "probs_done"))
        pt_done, pt_hi_done, pt_lo_done = sem("pt_done"), sem("pt_hi_done"), sem("pt_lo_done")
        pv_done, o_hi_done, o_lo_done = sem("pv_done"), sem("o_hi_done"), sem("o_lo_done")
        job_done, job_hi_done, job_lo_done = sem("job_done"), sem("job_hi_done"), sem("job_lo_done")
        x_res_in, out_t_done, out_added, out_stored = (
            sem(s) for s in ("x_res_in", "out_t_done", "out_added", "out_stored"))
        x_res = q_all[:, 0:NT * DM // SEQ].rearrange("p a r c -> p (a r c)")
        RES = 2 * DM
        ALL = BATCH * HEADS * TILES
        block = c.enter_context(nc.Block())

        JOBS = ["K0", "K1", "V0", "O0a", "O0b", "V1", "Vt0", "O1a", "O1b", "Vt1"]
        ON_SCALAR = ["K0", "K1", "V0", "V1", "Vt0", "Vt1"]
        ON_VECTOR = ["K0", "K1", "O0a", "O0b", "Vt0", "O1a", "O1b", "Vt1"]
        FIRST_AT = {0: "K0", 2: "O0a", 6: "O1b", 7: "Vt1"}
        EARLY_AT = {1: "K1", 3: "O0b", 5: "O1a"}
        LATE_AT = {1: "V0", 3: "V1", 4: "Vt0"}
        EAGER = (1, 3, 7)
        FIRST_JOBS = ON_SCALAR
        OUTPUTS = ["O0a", "O0b", "O1a", "O1b"]
        chunk_of = lambda i: i if i < QT else 2 * i - QT
        banks_of = lambda i: 1 if i < QT else 2

        class Pair:

            def __init__(self, o, p):
                self.o, self.p = o, p
                self.first = isinstance(p, int) and p == 0

            def count(self, k, c):
                if self.first and c <= 0:
                    return 0
                return self.o * (GROUP * k) + self.p * (2 * k) + c

            def head(self, par):
                return self.o * GROUP + self.p * 2 + par

            def shift(self, par, job):
                if not (self.first and par == 0):
                    return 0
                return sum(other[0] == "O" for other in JOBS[JOBS.index(job) + 1:])

            def jobs(self, par, job):
                return self.count(len(JOBS), par * len(JOBS) + len(ON_SCALAR) - len(OUTPUTS) + JOBS.index(job) + 1
                                  + self.shift(par, job))

            def hi(self, par, job):
                return self.count(len(ON_SCALAR), (par + 1) * len(ON_SCALAR) + ON_SCALAR.index(job) + 1)

            def lo(self, par, job, before=0):
                return self.count(len(ON_VECTOR), par * len(ON_VECTOR) + 4 - len(OUTPUTS) + ON_VECTOR.index(job) + 1
                                  + self.shift(par, job) - before)

        class Drain(Pair):

            def __init__(self):
                self.o, self.p, self.first = GROUPS - 1, PAIRS, False

            def jobs(self, par, job):
                return self.count(len(JOBS), len(ON_SCALAR) - len(OUTPUTS) + OUTPUTS.index(job) + 1)

            def lo(self, par, job, before=0):
                return self.count(len(ON_VECTOR), 4 - len(OUTPUTS) + OUTPUTS.index(job) + 1 - before)

        def lagging(b, t, lag):
            return None if b.first and t < lag else divmod(t - lag, TILES)

        def loops(eng, group_start, pair, drain):
            group_start(0)
            pair(Pair(0, 0))
            with eng.Fori(1, PAIRS) as p:
                pair(Pair(0, p))
            with eng.Fori(1, GROUPS) as o:
                group_start(o)
                with eng.Fori(0, PAIRS) as p:
                    pair(Pair(o, p))
            drain(Drain())

        def q_loop(eng, body):
            for u in range(4):
                body(0, u)
            with eng.Fori(1, HEADS // 4) as four:
                for u in range(4):
                    body(four * 4, u)

        def acc_cols(head, half):
            return bass.ds(((head >> 4) & (BATCH - 1)) * SEQ + half * N, N)

        @block.sync
        def _(sp):
            sp.wait_ge(q_lo_done, GROUPS * SPLITS)
            sp.dma_start(x_res.rearrange("p (t k) -> p t k", k=DM), d["x"].rearrange("(t p) k -> p t k", p=P)
                         ).then_inc(x_res_in, 16)
            for g in range(NT // 2):
                sp.wait_ge(out_added, g + 1)
                sp.dma_start(out.rearrange("(t p) k -> p t k", p=P)[:, 2 * g:2 * g + 2, :],
                             x_res[:, g * RES:(g + 1) * RES].rearrange("p (t k) -> p t k", k=DM)
                             ).then_inc(out_stored, 16)
            sp.wait_ge(out_stored, 16 * (NT // 2))

        @block.scalar
        def _(act):
            def load_wo(head):
                act.dma_start(wo_in[:], d["wo"][bass.ds((head & (HEADS - 1)) * DH, DH), :]).then_inc(wo_loaded, 16)

            def wo_high(n16, slot):
                act.wait_ge(wo_loaded, n16)
                nc.scalar.activation(wo_hi[:, slot, :], wo_in[:], ACT.Copy).then_inc(wo_hi_done, 1)

            def set_bias(now, bias, head, par):
                nc.scalar.activation(now[:, par:par + 1], bias[:, bass.ds(head & (HEADS - 1), 1)], ACT.Copy
                                     ).then_inc(bias_set, 1)

            act.wait_ge(bias_in, 48)
            set_bias(bk_now, bk, 0, 0)
            set_bias(bk_now, bk, 1, 1)
            act.wait_ge(bias_set, 2)

            def evacuate(job, jobs, par):
                act.wait_ge(job_done, jobs)
                half = int(job[-1])
                if job[0] == "K":
                    ins = nc.scalar.activation(k_hi[:, par, half * N:(half + 1) * N], M, ACT.Identity,
                                               bias=bk_now[:, par:par + 1])
                elif job in ("V0", "V1"):
                    ins = nc.scalar.activation(v_t[:, half, :], M, ACT.Copy)
                else:
                    ins = nc.scalar.activation(flat(v_hi[:, par, half * QT:(half + 1) * QT, :]), M, ACT.Copy)
                ins.then_inc(job_hi_done, 1)

            def q_split(m, half):
                rows = q_all[:, bass.ds(m, 1), half * 32:half * 32 + 32, :].rearrange("p a r c -> p (a r c)")
                nc.scalar.activation(q_hi[:, half, :], rows, ACT.Copy).then_inc(q_hi_done, 1)

            def wq_high(before, slot, loads, block_):
                act.wait_ge(wq_loaded[slot], loads)
                wait(act, qp_done, before + (1 - LOADS))
                nc.scalar.activation(flat(wq_hi[:, slot, :, :]), flat(wq_in[:, slot, :, :]), ACT.Copy
                                     ).then_inc(wq_hi_done, 1)
                wait(act, wq_lo_done, before)
                load_wq(act, sh, d, block_ + WQ_AHEAD, (slot + WQ_AHEAD) % LOADS)

            def group_start(o):
                if isinstance(o, int):
                    for n in range(WQ_AHEAD):
                        wq_high(n, n, 16, n)
                    evacuate("K0", 1, 0)
                    act.wait_ge(kv_lo_done, 1)
                    load_kv(act, sh, d, 1)
                    load_wo(0)

                def wq_block(before, u):
                    rounds = 1 + (u + WQ_AHEAD) // LOADS
                    wq_high(o * HEADS + (before + (u + WQ_AHEAD)), (u + WQ_AHEAD) % LOADS,
                            (o * HEADS + before) * (16 // LOADS) + 16 * rounds, before + (u + WQ_AHEAD))
                    if isinstance(o, int) and isinstance(before, int):
                        evacuate(FIRST_JOBS[u + 1], u + 2, 0)
                        if FIRST_JOBS[u + 1] == "V1":
                            kv_high(nc, act, sh, 64)
                q_loop(act, wq_block)
                if isinstance(o, int):
                    evacuate("Vt1", 6, 0)
                act.wait_ge(q_done, o * HEADS + HEADS)
                q_split(0, 0)

            def pt_high(b, par, i):
                for ch in range(banks_of(i)):
                    at = chunk_of(i) + ch
                    blocks = min(QT, i + 1 - ch * QT)
                    act.wait_ge(pt_done, b.count(CHUNKS, par * CHUNKS + at + 1))
                    nc.scalar.activation(
                        pt_hi[:, i // 2 % 2, ch * QT:ch * QT + blocks, i % 2 * P:(i % 2 + 1) * P],
                        T[at % 2][:, 0:blocks * P].rearrange("p (a b) -> p a b", b=P), ACT.Copy
                    ).then_inc(pt_hi_done, 1)

            def o_high(b, par, half):
                act.wait_ge(pv_done, b.count(4, par * 4 + 2 * half + 2))
                nc.scalar.activation(o_hi[:], O, ACT.Identity, bias=bv_now[:, par % 2:par % 2 + 1]
                                     ).then_inc(o_hi_done, 1)

            def exps(b, t):
                act.wait_ge(max_done, b.count(TILES, t + 1))
                width = (t % TILES + 1) * P
                nc.scalar.activation(probs[:, t % 4, 0:width], flat(S[t % 2])[:, 0:width], ACT.Exp,
                                     bias=neg_max[:, t:t + 1], accum_out=row_sum[:, t:t + 1]
                                     ).then_inc(exp_done, 1)

            def pair(b):
                for t in range(2 * TILES):
                    par, i = divmod(t, TILES)
                    if i - 1 in LATE_AT:
                        evacuate(LATE_AT[i - 1], b.jobs(par, LATE_AT[i - 1]), 1 - par)
                    if lagging(b, t, LAG):
                        pt_high(b, *lagging(b, t, LAG))
                    if FIRST_AT.get(i) in ON_SCALAR:
                        evacuate(FIRST_AT[i], b.jobs(par, FIRST_AT[i]), 1 - par)
                    if i in (0, 4) and not (b.first and par == 0):
                        o_high(b, par - 1, i // 4)
                    if i > 0 and i - 1 not in EAGER:
                        exps(b, t - 1)
                    if EARLY_AT.get(i) in ON_SCALAR:
                        evacuate(EARLY_AT[i], b.jobs(par, EARLY_AT[i]), 1 - par)
                    if i == 1:
                        act.wait_ge(scores_done, b.count(TILES, t))
                        q_split(b.p * 2 + par, 1)
                    if i == 2:
                        wo_high(b.count(16, par * 16 + 16), par)
                    if i == 5:
                        act.wait_ge(scores_done, b.count(TILES, t))
                        q_split((b.p * 2 + (par + 1)) & (GROUP - 1), 0)
                        set_bias(bk_now, bk, b.head(par + 2), par)
                        set_bias(bv_now, bv, b.head(par), par)
                    if i == 6:
                        act.wait_ge(bias_set, b.count(2, par * 2 + 4))
                        kv_high(nc, act, sh, b.count(32, par * 32 + 96))
                    if i in EAGER:
                        exps(b, t)
                    if i == 3:
                        act.wait_ge(kv_lo_done, b.count(1, par + 2))
                        load_kv(act, sh, d, b.head(par + 2))
                        act.wait_ge(wo_lo_done, b.count(1, par + 1))
                        load_wo(b.head(par + 1))

            def drain(b):
                pt_high(b, -1, 5)
                o_high(b, -1, 0)
                pt_high(b, -1, 6)
                pt_high(b, -1, 7)
                o_high(b, -1, 1)
            loops(act, group_start, pair, drain)
            act.wait_ge(kv_loaded, 32 * (BATCH * HEADS + 2))
            act.wait_ge(wo_loaded, 16 * (BATCH * HEADS + 1))
            for s in range(LOADS):
                act.wait_ge(wq_loaded[s], 16 * ((GROUPS * HEADS + 2 * WQ_AHEAD - s + LOADS - 1) // LOADS))

        @block.gpsimd
        def _(pool):
            def low(dst, src, high, high_done, count, done):
                pool.wait_ge(high_done, count)
                nc.gpsimd.tensor_tensor(dst, src, high.bitcast(F32), ALU.subtract).then_inc(done, 1)

            def wo_low(count, slot):
                low(wo_lo[:, slot, :], wo_in[:], wo_hi[:, slot, :], wo_hi_done, count, wo_lo_done)

            def q_low(m, half, count):
                rows = q_all[:, bass.ds(m, 1), half * 32:half * 32 + 32, :].rearrange("p a r c -> p (a r c)")
                low(q_lo[:, half, :], rows, q_hi[:, half, :], q_hi_done, count, q_lo_done)


            def group_start(o):
                if isinstance(o, int):
                    kv_low(nc, pool, sh, 2)

            def pair(b):
                splits = lambda par, half: b.o * SPLITS + b.p * 4 + (2 * par + half + 1)
                for t in range(2 * TILES):
                    par, i = divmod(t, TILES)
                    pool.wait_ge(exp_done, b.count(TILES, t + 1))
                    nc.gpsimd.tensor_tensor(inv_sum[:, t:t + 1], row_sum[:, t:t + 1], minus_one[:], ALU.pow
                                            ).then_inc(inv_done, 1)
                    pool.wait_ge(inv_done, b.count(TILES, t + 1))
                    row = probs[:, t % 4, 0:(i + 1) * P]
                    nc.gpsimd.tensor_tensor(row, row, inv_sum[:, t:t + 1].to_broadcast([P, (i + 1) * P]),
                                            ALU.mult).then_inc(probs_done, 1)
                    if i == 0:
                        q_low(b.p * 2 + par, 1, splits(par, 1))
                    if i == 2:
                        wo_low(b.count(1, par + 1), par)
                    if i == 4:
                        q_low((b.p * 2 + (par + 1)) & (GROUP - 1), 0, splits(par, 2))
                    if i == 5:
                        kv_low(nc, pool, sh, b.count(1, par + 3))
            loops(pool, group_start, pair, lambda b: None)

        @block.vector
        def _(dve):
            dve.wait_ge(bias_in, 48)

            def evacuate(job, jobs, hi, head, par):
                if hi is not None:
                    dve.wait_ge(job_hi_done, hi)
                half = int(job[-1]) if job[0] != "O" else int(job[1])
                if job[0] == "K":
                    cols = slice(half * N, (half + 1) * N)
                    ins = nc.vector.scalar_tensor_tensor(
                        k_lo[:, par, cols], M, bk_now[:, par:par + 1],
                        k_hi[:, par, cols].bitcast(F32), ALU.add, ALU.subtract)
                elif job[0] == "V":
                    blocks = slice(half * QT, (half + 1) * QT)
                    ins = nc.vector.tensor_tensor(flat(v_lo[:, par, blocks, :]), M,
                                                  flat(v_hi[:, par, blocks, :]).bitcast(F32), ALU.subtract)
                else:
                    dve.wait_ge(job_done, jobs)
                    cols = acc[:, "ab".index(job[2]), acc_cols(head, half)]
                    ins = nc.vector.tensor_tensor(cols, M, cols, ALU.add)
                ins.then_inc(job_lo_done, 1)

            def group_start(o):
                def wq_low(block_, slot):
                    dve.wait_ge(wq_hi_done, block_ + 1)
                    nc.vector.tensor_tensor(
                        flat(wq_lo[:, slot, :, :]), flat(wq_in[:, slot, :, :]), flat(wq_hi[:, slot, :, :]).bitcast(F32),
                        ALU.subtract).then_inc(wq_lo_done, 1)

                if isinstance(o, int):
                    for n in range(WQ_AHEAD):
                        wq_low(n, n)
                    evacuate("K0", None, 1, 0, 0)

                def q_block(before, u):
                    wq_low(o * HEADS + (before + (u + WQ_AHEAD)), (u + WQ_AHEAD) % LOADS)
                    if isinstance(before, int) and u == 0:
                        wait(dve, q_lo_done, o * SPLITS)
                    dve.wait_ge(qp_done, o * HEADS + (before + (u + 1)))
                    dst = q_all[:].rearrange("p m r c -> p (m r) c")[:, :, bass.ds(before + u, 1)]
                    nc.vector.tensor_scalar(
                        dst.rearrange("p a b -> p (a b)"), S[u % 2][:, 0, :], bq[:, bass.ds(before + u, 1)],
                        SCALE, ALU.add, ALU.mult).then_inc(q_done, 1)
                    if isinstance(o, int) and isinstance(before, int) and FIRST_JOBS[u + 1] in ON_VECTOR:
                        evacuate(FIRST_JOBS[u + 1], None, u + 2, 0, 0)
                q_loop(dve, q_block)
                if isinstance(o, int):
                    evacuate("Vt1", None, 6, 0, 0)
                dve.wait_ge(q_hi_done, o * SPLITS + 1)
                nc.vector.tensor_tensor(q_lo[:, 0, :], q_all[:, 0, 0:32, :].rearrange("p r c -> p (r c)"),
                                        q_hi[:, 0, :].bitcast(F32), ALU.subtract).then_inc(q_lo_done, 1)

            def pt_low(b, par, i, ch):
                at = chunk_of(i) + ch
                blocks = min(QT, i + 1 - ch * QT)
                dve.wait_ge(pt_hi_done, b.count(CHUNKS, par * CHUNKS + at + 1))
                where = (slice(None), i // 2 % 2, slice(ch * QT, ch * QT + blocks), slice(i % 2 * P, (i % 2 + 1) * P))
                nc.vector.tensor_tensor(pt_lo[where], T[at % 2][:, 0:blocks * P].rearrange("p (a b) -> p a b", b=P),
                                        pt_hi[where].bitcast(F32), ALU.subtract).then_inc(pt_lo_done, 1)

            def o_low(b, par, half):
                dve.wait_ge(o_hi_done, b.count(2, par * 2 + half + 1))
                nc.vector.scalar_tensor_tensor(o_lo[:], O, bv_now[:, par % 2:par % 2 + 1],
                                               o_hi[:].bitcast(F32), ALU.add, ALU.subtract).then_inc(o_lo_done, 1)

            def pair(b):
                for t in range(2 * TILES):
                    par, i = divmod(t, TILES)
                    follows = not (b.first and par == 0)

                    def take_out(name):
                        if name in ON_VECTOR and name[0] != "O":
                            evacuate(name, None, b.hi(par, name), None, 1 - par)
                        elif name in ON_VECTOR and follows:
                            evacuate(name, b.jobs(par, name), None, b.head(par - 1), None)

                    between = FIRST_AT.get(i) == "O0a"
                    if lagging(b, t, LAG):
                        tile = lagging(b, t, LAG)
                        pt_low(b, *tile, 0)
                        if between:
                            take_out(FIRST_AT[i])
                        if banks_of(tile[1]) > 1:
                            pt_low(b, *tile, 1)
                    if not between:
                        take_out(FIRST_AT.get(i))
                    if i in (0, 4) and follows:
                        o_low(b, par - 1, i // 4)
                    if i == 4:
                        take_out(LATE_AT[i])
                    hurry = EARLY_AT.get(i) == "O1a"
                    if hurry:
                        take_out(EARLY_AT[i])
                    dve.wait_ge(scores_done, b.count(TILES, t + 1))
                    nc.vector.tensor_reduce(neg_max[:, t:t + 1], flat(S[t % 2])[:, 0:(i + 1) * P], AX.X, ALU.max,
                                            negate=True).then_inc(max_done, 1)
                    if not hurry:
                        take_out(EARLY_AT.get(i))

            def add_residual(g):
                if g == 0:
                    dve.wait_ge(x_res_in, 16)
                dve.wait_ge(out_t_done, g + 1)
                cols = x_res[:, g * RES:(g + 1) * RES]
                nc.vector.tensor_tensor(cols, ps[:, g % 4, :], cols, ALU.add).then_inc(out_added, 1)

            def drain(b):
                def output(job):
                    evacuate(job, b.jobs(0, job), None, b.head(-1), None)

                def pt_lows(i):
                    for ch in range(banks_of(i)):
                        pt_low(b, -1, i, ch)

                pt_lows(5)
                o_low(b, -1, 0)
                add_residual(0)
                add_residual(1)
                output("O0a")
                pt_lows(6)
                add_residual(2)
                output("O0b")
                pt_lows(7)
                add_residual(3)
                add_residual(4)
                o_low(b, -1, 1)
                output("O1a")
                add_residual(5)
                output("O1b")
                add_residual(6)
                add_residual(7)
            loops(dve, group_start, pair, drain)

        @block.tensor
        def _(pe):
            pe.wait_ge(sh["masks_made"], 2)

            def project(job, head, weights):
                cols = bass.ds(((head >> 4) & (BATCH - 1)) * SEQ + int(job[1]) * N, N)
                part = slice(0, DH) if job[0] == "K" else slice(DH, 2 * DH)
                pe.wait_ge(kv_lo_done, weights)
                for ch in range(KC):
                    last = split_matmul(nc, M, kv_hi[:, ch, part], kv_lo[:, ch, part], xn_hi[:, ch, cols],
                                        xn_lo[:, ch, cols], ch == 0, ch == KC - 1)
                return last

            def v_rows(half):
                for t in range(QT):
                    last = nc.tensor.transpose(M[:, t * P:(t + 1) * P], v_t[:, half, t * P:(t + 1) * P], ident[:])
                return last

            def first_job(n):
                job = FIRST_JOBS[n]
                if n > 0 and FIRST_JOBS[n - 1] in ("V0", "V1"):
                    pe.wait_ge(job_hi_done, n)
                elif n > 0:
                    pe.wait_ge(job_lo_done, sum(other in ON_VECTOR for other in FIRST_JOBS[:n]))
                last = v_rows(int(job[-1])) if job[:2] == "Vt" else project(job, 0, 1)
                last.then_inc(job_done, 1)

            def group_start(o):
                if isinstance(o, int):
                    first_job(0)

                def q_block(before, u):
                    if isinstance(before, int) and u < 2:
                        wait(pe, exp_done, o * GROUP * TILES - (1 - u))
                    pe.wait_ge(wq_lo_done, o * HEADS + (before + (u + 1)))
                    if not (isinstance(before, int) and u < 2):
                        pe.wait_ge(q_done, o * HEADS + (before + (u - 1)))
                    cols = bass.ds(o * N, N)
                    for ch in range(KC):
                        last = split_matmul(nc, S[u % 2][:, 0, :], wq_hi[:, u, ch, :], wq_lo[:, u, ch, :],
                                            xn_hi[:, ch, cols], xn_lo[:, ch, cols], ch == 0, ch == KC - 1)
                    last.then_inc(qp_done, 1)
                    if isinstance(o, int) and isinstance(before, int):
                        first_job(u + 1)
                q_loop(pe, q_block)
                if isinstance(o, int):
                    first_job(len(FIRST_JOBS) - 1)

            def scores(b, t):
                par, i = divmod(t, TILES)
                if i == 0 and b.first and par == 0:
                    pe.wait_ge(job_lo_done, b.count(len(ON_VECTOR), 4))
                elif i == 0:
                    pe.wait_ge(job_lo_done, b.lo(par - 1, "K1"))
                if i % QT == 0:
                    pe.wait_ge(q_lo_done, b.o * SPLITS + b.p * 4 + (2 * par + i // QT + 1))
                wait(pe, exp_done, b.count(TILES, t - 1))
                half, cols = i // QT, slice(i % QT * P, (i % QT + 1) * P)
                for bank in range(i // QT + 1):
                    width = min(N, (i + 1) * P - bank * N)
                    keys = slice(bank * N, bank * N + width)
                    diagonal = bank == i // QT
                    last = split_matmul(nc, S[t % 2][:, bank, 0:width], q_hi[:, half, cols], q_lo[:, half, cols],
                                        k_hi[:, par, keys], k_lo[:, par, keys], True, not diagonal)
                    if diagonal:
                        last = nc.tensor.matmul(S[t % 2][:, bank, cols], ident_b[:], mask_b[:], start=False, stop=True)
                last.then_inc(scores_done, 1)

            def transposes(b, par, i, slot):
                pe.wait_ge(probs_done, b.count(TILES, par * TILES + i + 1))
                for ch in range(banks_of(i)):
                    at = chunk_of(i) + ch
                    wait(pe, pt_lo_done, b.count(CHUNKS, par * CHUNKS + at - 1))
                    for n in range(min(QT, i + 1 - ch * QT)):
                        s = ch * QT + n
                        last = nc.tensor.transpose(T[at % 2][:, n * P:(n + 1) * P], probs[:, slot, s * P:(s + 1) * P],
                                                   ident[:])
                    last.then_inc(pt_done, 1)

            def with_v(b, par, q):
                pe.wait_ge(pt_lo_done, b.count(CHUNKS, par * CHUNKS + chunk_of(2 * q + 1) + banks_of(2 * q + 1)))
                if q % 2 == 0:
                    wait(pe, o_lo_done, b.count(2, par * 2 + q // 2))
                for s in range(2 * q + 2):
                    first = P if s == 2 * q + 1 else 0
                    out = O[:, q % 2 * QUARTER + first:(q % 2 + 1) * QUARTER]
                    last = split_matmul(nc, out, v_hi[:, par % 2, s, :], v_lo[:, par % 2, s, :],
                                        pt_hi[:, q % 2, s, first:], pt_lo[:, q % 2, s, first:], s == 0, s == 2 * q + 1)
                last.then_inc(pv_done, 1)

            def output(b, par, half, h):
                pe.wait_ge(o_lo_done, b.count(2, par * 2 + half + 1))
                cols = slice(h * P, (h + 1) * P)
                slot = par % 2
                return split_matmul(nc, M, wo_hi[:, slot, cols], wo_lo[:, slot, cols], o_hi[:], o_lo[:], True, True)

            def job(b, par, name):
                if name is None or (b.first and par == 0 and name in OUTPUTS):
                    return
                before = [other for other in JOBS[:JOBS.index(name)]
                          if not (b.first and par == 0 and other[0] == "O")]
                if isinstance(b, Drain) or not before:
                    pe.wait_ge(job_lo_done, b.lo(par, name, before=1))
                elif before[-1] in ("V0", "V1"):
                    pe.wait_ge(job_hi_done, b.hi(par, before[-1]))
                else:
                    pe.wait_ge(job_lo_done, b.lo(par, before[-1]))
                if name in ("K0", "K1", "V0", "V1"):
                    last = project(name, b.head(par + 1), b.count(1, par + 2))
                elif name in ("Vt0", "Vt1"):
                    last = v_rows(int(name[-1]))
                else:
                    if name == "O0a":
                        pe.wait_ge(wo_lo_done, b.count(1, par))
                    last = output(b, par - 1, int(name[1]), "ab".index(name[2]))
                last.then_inc(job_done, 1)

            def pair(b):
                for t in range(2 * TILES):
                    par, i = divmod(t, TILES)
                    if lagging(b, t, LAG):
                        transposes(b, *lagging(b, t, LAG), (t - LAG) % 4)
                    job(b, par, FIRST_AT.get(i))
                    scores(b, t)
                    job(b, par, EARLY_AT.get(i))
                    if t % 2 == 1 and lagging(b, t, LAG + 2):
                        at = lagging(b, t, LAG + 2)
                        with_v(b, at[0], at[1] // 2)
                    job(b, par, LATE_AT.get(i))

            def to_rows(g):
                if g < 4:
                    pe.wait_ge(exp_done, ALL - (g < 2))
                else:
                    pe.wait_ge(out_added, g - 3)
                for t in range(2):
                    for h in range(KC):
                        last = nc.tensor.transpose(ps[:, g % 4, (2 * t + h) * P:(2 * t + h + 1) * P],
                                                   acc[:, h, (2 * g + t) * P:(2 * g + t + 1) * P], ident[:])
                last.then_inc(out_t_done, 1)

            def drain(b):
                transposes(b, -1, 5, 5 % 4)
                to_rows(0)
                to_rows(1)
                job(b, 0, "O0a")
                transposes(b, -1, 6, 6 % 4)
                to_rows(2)
                job(b, 0, "O0b")
                with_v(b, -1, 2)
                transposes(b, -1, 7, 7 % 4)
                to_rows(3)
                pe.wait_ge(job_lo_done, b.lo(0, "O0b"))
                to_rows(4)
                with_v(b, -1, 3)
                job(b, 0, "O1a")
                to_rows(5)
                job(b, 0, "O1b")
                pe.wait_ge(job_lo_done, b.lo(0, "O1b"))
                to_rows(6)
                to_rows(7)
            loops(pe, group_start, pair, drain)


def layer(nc, d, out):
    with ExitStack() as c:
        sb = lambda name, shape, dt: c.enter_context(nc.sbuf_tensor(name, shape, dt))
        sh = {
            "xn_hi": sb("xn_hi", [P, KC, TOK], F32R), "xn_lo": sb("xn_lo", [P, KC, TOK], F32R),
            "acc": sb("acc", [P, KC, TOK], F32), "ident": sb("ident", [P, P], F32),
            "ps": c.enter_context(nc.psum_tensor("ps", [P, 8, N], F32)),
        }
        sem = lambda name: c.enter_context(nc.semaphore(name))
        for name, shape, dt in (("kv_in", [P, KC, 2 * DH], F32), ("kv_hi", [P, KC, 2 * DH], F32R),
                                ("kv_lo", [P, KC, 2 * DH], F32R), ("wq_in", [P, LOADS, KC, DH], F32),
                                ("ident_b", [P, P], BF16), ("mask_b", [P, P], BF16), ("minus_one", [P, 1], F32),
                                ("bq", [P, HEADS], F32), ("bk", [P, HEADS], F32), ("bv", [P, HEADS], F32)):
            sh[name] = sb(name, shape, dt)
        for name in ("kv_loaded", "kv_hi_done", "kv_lo_done", "bias_in", "masks_zeroed", "masks_made"):
            sh[name] = sem(name)
        sh["wq_loaded"] = [sem(f"wq_loaded{s}") for s in range(LOADS)]
        norm_and_ffn(nc, sh, d)
        attention(nc, sh, d, out)


def kernel(**inputs):
    import concourse.bacc as bacc
    from concourse.bass_utils import run_bass_kernel_spmd

    names = {
        "x": ("L0_attn_x", (TOK, DM)), "wq": ("L0_attn_Wq", None), "bq": ("L0_attn_bq", None),
        "wk": ("L0_attn_Wk", None), "bk": ("L0_attn_bk", None), "wv": ("L0_attn_Wv", None),
        "bv": ("L0_attn_bv", None), "wo": ("L0_attn_Wo", None), "bo": ("L0_attn_bo", None),
        "gate": ("L0_ffn_gate_W_packed", None), "gate_scales": ("L0_ffn_gate_scales", None),
        "up": ("L0_ffn_up_W_packed", None), "up_scales": ("L0_ffn_up_scales", None),
        "down": ("L0_ffn_down_W_packed", None), "down_scales": ("L0_ffn_down_scales", None),
    }
    nc = bacc.Bacc("TRN2", target_bir_lowering=False, num_devices=1)
    arrays, d = {}, {}
    for short, (name, shape) in names.items():
        a = np.ascontiguousarray(inputs[name])
        if shape is not None:
            a = a.reshape(shape)
        elif a.ndim == 1:
            a = np.ascontiguousarray(a.reshape(-1, P).T)
        arrays[f"in_{short}"] = a
        d[short] = nc.dram_tensor(f"in_{short}", a.shape, mybir.dt.from_np(a.dtype), kind="ExternalInput").ap()
    out = nc.dram_tensor("out", (TOK, DM), F32, kind="ExternalOutput").ap()
    layer(nc, d, out)
    result = run_bass_kernel_spmd(nc, [arrays], core_ids=[0])
    return np.asarray(result.results[0]["out"]).reshape(BATCH, SEQ, DM)
```
